# Optimizing a Trainium2 kernel written in Bass

```python
import numpy as np
import jax
import jax.numpy as jnp

def _softmax(x, axis=-1):
    return jax.nn.softmax(x, axis=axis)

def _gelu(x):
    return jax.nn.gelu(x, approximate=True)

def _silu(x):
    return jax.nn.silu(x)

def _sigmoid(x):
    return jax.nn.sigmoid(x)

def _layernorm(x, axis=-1, eps=1e-05):
    m = jnp.mean(x, axis=axis, keepdims=True)
    v = jnp.var(x, axis=axis, keepdims=True)
    return (x - m) / jnp.sqrt(v + eps)

def _scatter_add(tgt, idx, src, axis=0):
    return tgt.at[idx].add(src)

def _segment_sum(src, seg, n):
    return jax.ops.segment_sum(src, seg, n)
kernel_name = 'mk_cond_seq_d1_seqx_r8_cb1afa'

def setup_inputs(seed: int=0):
    np.random.seed(seed)
    _w = jnp.asarray

    def _rec_inputs():
        import jax
        import jax.numpy as jnp
        _rk = jax.random.key(seed)
        x = -0.0002928 + 1 * jax.random.normal(jax.random.fold_in(_rk, 1), (8, 256, 128), jnp.float32)
        _lenS = 256 - jax.random.randint(jax.random.fold_in(_rk, 7), (8,), 0, max(1, 256 // 4) + 1, jnp.int32)
        _lenS2 = 256 - jax.random.randint(jax.random.fold_in(_rk, 8), (8,), 0, max(1, 256 // 4) + 1, jnp.int32)
        cond_1024 = 0.000887014 + 1.03683 * jax.random.normal(jax.random.fold_in(_rk, 11), (8, 128), jnp.float32)
        _validS = jnp.arange(256)[None, :] < _lenS[:, None]
        _validS2 = jnp.arange(256)[None, :] < _lenS2[:, None]
        _causal = jnp.tril(jnp.ones((256, 256), dtype=bool))
        mask_BxS_ik0 = jnp.where(jnp.broadcast_to(_validS[:, :], (8, 256)), 0, 1).astype(jnp.int32)
        return (x, cond_1024, mask_BxS_ik0)
    x, cond_1024, mask_BxS_ik0 = _rec_inputs()

    def _L0_cond_setup():
        import jax, jax.numpy as jnp
        import numpy as np
        EMBED = 128
        HEADS = 16
        HEAD_DIM = EMBED // HEADS
        MLP = 4 * EMBED
        EPS = 1e-06

        def _adaln(x, c, norm_w, scale_w, scale_b, shift_w, shift_b):
            sc = jax.nn.silu(c)
            shift = sc @ shift_w.T + shift_b
            scale = jnp.clip(sc @ scale_w.T + scale_b + 1.0, 0.1, 10.0)
            norm = jnp.maximum(jnp.linalg.norm(x, axis=-1, keepdims=True) * x.shape[-1] ** (-0.5), EPS)
            h = x / norm * norm_w
            return h * scale[:, None, :] + shift[:, None, :]

        def _attention(x, attention_mask, qkv_w, proj_w, proj_b):
            B, N, C = x.shape
            qkv = (x @ qkv_w.T).reshape(B, N, 3, HEADS, HEAD_DIM)
            q = qkv[:, :, 0].transpose(0, 2, 1, 3)
            k = qkv[:, :, 1].transpose(0, 2, 1, 3)
            v = qkv[:, :, 2].transpose(0, 2, 1, 3)
            attn = jnp.einsum('bhnd,bhmd->bhnm', q, k) * HEAD_DIM ** (-0.5)
            mask = attention_mask[:, None, None, :]
            attn = jnp.where(mask == 0, -jnp.inf, attn)
            all_inf = jnp.all(attn == -jnp.inf, axis=-1, keepdims=True)
            attn = jnp.where(all_inf, 0.0, attn)
            p = jax.nn.softmax(attn, axis=-1)
            out = jnp.einsum('bhnm,bhmd->bhnd', p, v).transpose(0, 2, 1, 3).reshape(B, N, C)
            return out @ proj_w.T + proj_b

        def _mlp(x, w1, b1, w2, b2):
            h = x @ w1.T + b1
            x1, x2 = jnp.split(h, 2, axis=-1)
            return jax.nn.silu(x1) * x2 @ w2.T + b2
        key = jax.random.key(seed)
        ks = jax.random.split(key, 16)
        B, N, C = (2, 256, EMBED)
        x = jax.random.normal(ks[0], (B, N, C), dtype=jnp.float32)
        c = jax.random.normal(ks[1], (B, C), dtype=jnp.float32)
        attention_mask = jax.random.randint(ks[2], (B, N), 0, 2, dtype=jnp.int32)
        s = 0.02
        params = {'norm_w': jnp.ones((C,), jnp.float32), 'scale_w': s * jax.random.normal(ks[3], (C, C), jnp.float32), 'scale_b': s * jax.random.normal(ks[4], (C,), jnp.float32), 'shift_w': s * jax.random.normal(ks[5], (C, C), jnp.float32), 'shift_b': s * jax.random.normal(ks[6], (C,), jnp.float32), 'qkv_w': s * jax.random.normal(ks[7], (3 * C, C), jnp.float32), 'proj_w': s * jax.random.normal(ks[8], (C, C), jnp.float32), 'proj_b': s * jax.random.normal(ks[9], (C,), jnp.float32), 'mlp_w1': s * jax.random.normal(ks[10], (2 * MLP, C), jnp.float32), 'mlp_b1': s * jax.random.normal(ks[11], (2 * MLP,), jnp.float32), 'mlp_w2': s * jax.random.normal(ks[12], (C, MLP), jnp.float32), 'mlp_b2': s * jax.random.normal(ks[13], (C,), jnp.float32)}
        return {'x': x, 'c': c, 'attention_mask': attention_mask, **params}
    _L0_cond_all = _L0_cond_setup()
    _L0_cond_in = {k: v for k, v in _L0_cond_all.items() if k in ('norm_w', 'scale_w', 'scale_b', 'shift_w', 'shift_b', 'qkv_w', 'proj_w', 'proj_b', 'mlp_w1', 'mlp_b1', 'mlp_w2', 'mlp_b2')}
    del _L0_cond_all
    return {'x': x, 'cond_1024': cond_1024, 'mask_BxS_ik0': mask_BxS_ik0, 'L0_cond_norm_w': _L0_cond_in['norm_w'], 'L0_cond_scale_w': _L0_cond_in['scale_w'], 'L0_cond_scale_b': _L0_cond_in['scale_b'], 'L0_cond_shift_w': _L0_cond_in['shift_w'], 'L0_cond_shift_b': _L0_cond_in['shift_b'], 'L0_cond_qkv_w': _L0_cond_in['qkv_w'], 'L0_cond_proj_w': _L0_cond_in['proj_w'], 'L0_cond_proj_b': _L0_cond_in['proj_b'], 'L0_cond_mlp_w1': _L0_cond_in['mlp_w1'], 'L0_cond_mlp_b1': _L0_cond_in['mlp_b1'], 'L0_cond_mlp_w2': _L0_cond_in['mlp_w2'], 'L0_cond_mlp_b2': _L0_cond_in['mlp_b2']}

def reference(x, cond_1024, mask_BxS_ik0, L0_cond_norm_w, L0_cond_scale_w, L0_cond_scale_b, L0_cond_shift_w, L0_cond_shift_b, L0_cond_qkv_w, L0_cond_proj_w, L0_cond_proj_b, L0_cond_mlp_w1, L0_cond_mlp_b1, L0_cond_mlp_w2, L0_cond_mlp_b2):
    import jax
    import jax.numpy as jnp

    def _L0_cond_ref(x, c, attention_mask, norm_w, scale_w, scale_b, shift_w, shift_b, qkv_w, proj_w, proj_b, mlp_w1, mlp_b1, mlp_w2, mlp_b2):
        import jax, jax.numpy as jnp
        import numpy as np
        EMBED = 128
        HEADS = 16
        HEAD_DIM = EMBED // HEADS
        MLP = 4 * EMBED
        EPS = 1e-06

        def _adaln(x, c, norm_w, scale_w, scale_b, shift_w, shift_b):
            sc = jax.nn.silu(c)
            shift = sc @ shift_w.T + shift_b
            scale = jnp.clip(sc @ scale_w.T + scale_b + 1.0, 0.1, 10.0)
            norm = jnp.maximum(jnp.linalg.norm(x, axis=-1, keepdims=True) * x.shape[-1] ** (-0.5), EPS)
            h = x / norm * norm_w
            return h * scale[:, None, :] + shift[:, None, :]

        def _attention(x, attention_mask, qkv_w, proj_w, proj_b):
            B, N, C = x.shape
            qkv = (x @ qkv_w.T).reshape(B, N, 3, HEADS, HEAD_DIM)
            q = qkv[:, :, 0].transpose(0, 2, 1, 3)
            k = qkv[:, :, 1].transpose(0, 2, 1, 3)
            v = qkv[:, :, 2].transpose(0, 2, 1, 3)
            attn = jnp.einsum('bhnd,bhmd->bhnm', q, k) * HEAD_DIM ** (-0.5)
            mask = attention_mask[:, None, None, :]
            attn = jnp.where(mask == 0, -jnp.inf, attn)
            all_inf = jnp.all(attn == -jnp.inf, axis=-1, keepdims=True)
            attn = jnp.where(all_inf, 0.0, attn)
            p = jax.nn.softmax(attn, axis=-1)
            out = jnp.einsum('bhnm,bhmd->bhnd', p, v).transpose(0, 2, 1, 3).reshape(B, N, C)
            return out @ proj_w.T + proj_b

        def _mlp(x, w1, b1, w2, b2):
            h = x @ w1.T + b1
            x1, x2 = jnp.split(h, 2, axis=-1)
            return jax.nn.silu(x1) * x2 @ w2.T + b2
        x = x + _attention(_adaln(x, c, norm_w, scale_w, scale_b, shift_w, shift_b), attention_mask, qkv_w, proj_w, proj_b)
        x = x + _mlp(_adaln(x, c, norm_w, scale_w, scale_b, shift_w, shift_b), mlp_w1, mlp_b1, mlp_w2, mlp_b2)
        return x
    x = _L0_cond_ref(x, cond_1024, mask_BxS_ik0, L0_cond_norm_w, L0_cond_scale_w, L0_cond_scale_b, L0_cond_shift_w, L0_cond_shift_b, L0_cond_qkv_w, L0_cond_proj_w, L0_cond_proj_b, L0_cond_mlp_w1, L0_cond_mlp_b1, L0_cond_mlp_w2, L0_cond_mlp_b2)
    return x

_drawn_inputs = setup_inputs


def setup_inputs(seed=0):
    import zlib

    import numpy as np

    out = dict(_drawn_inputs(seed))
    spreads = {'L0_cond_norm_w': (1.0, 0.6)}
    factors = {'cond_1024': 7.546,
     'L0_cond_scale_w': 8.0,
     'L0_cond_scale_b': 8.0,
     'L0_cond_shift_w': 7.469,
     'L0_cond_shift_b': 8.0,
     'L0_cond_qkv_w': 4.901,
     'L0_cond_proj_w': 4.794,
     'L0_cond_mlp_w1': 4.266,
     'L0_cond_mlp_b1': 25.884,
     'L0_cond_mlp_w2': 4.269,
     'L0_cond_mlp_b2': 176.32,
     'L0_cond_proj_b': 39.035}
    for name, (base, spread) in spreads.items():
        noise = np.random.default_rng([zlib.crc32(name.encode()), seed]).standard_normal(out[name].shape)
        drawn = base * np.exp(spread * noise) if base else spread * noise
        out[name] = jnp.asarray(drawn.astype(out[name].dtype))
    for name, factor in factors.items():
        out[name] = (out[name] * factor).astype(out[name].dtype)
    return out
```

```python
from contextlib import ExitStack

import concourse.bass as bass
from concourse import mybir

F32 = mybir.dt.float32
BF16 = mybir.dt.bfloat16
I32 = mybir.dt.int32
U32 = mybir.dt.uint32
ALU = mybir.AluOpType
ACT = mybir.ActivationFunctionType
AX = mybir.AxisListType

C = 128
B, N = 8, 256
TOK = B * N
H, D = 16, 8
MLP = 4 * C
G = H // 2
CH = 512
NC = TOK // CH
BC = CH // N
KT = N // 128
VW = D + 1
EPS = 1e-6
MASKED = -float(2 ** 100)
ONES_BF16 = 0x3F803F80

RUNS = [(0, 3), (3 * D, 2), (5 * D, 1)]
ROW_MASK = 6 * D
ROW_MAX = ROW_MASK + 1
HALVES = 2 * B
UNITS = B * G

V_NORM, V_SCALE_B, V_SHIFT_B, V_PROJ_B, V_B2, V_B1 = 0, 1, 2, 3, 4, 5
NVEC = V_B1 + 2 * MLP // C


def unit_item(u):
    return 2 * u + (max(u, 1) - 1) // 4


def turn_item(k):
    return min(2 * (4 * k + 5), 2 * UNITS) + k


def build(nc, x_t, c_t, mask, vecs, scale_wt, shift_wt, qkv_wt, proj_wt, w1_t, w2_t, out_t):
    q_parts = nc.dram_tensor("q_parts", [H, 3, D, TOK], BF16).ap()
    k_parts = nc.dram_tensor("k_parts", [H, 3, D, TOK], BF16).ap()
    o_rows = nc.dram_tensor("o_rows", [B, H, VW, N], F32).ap()

    ctx = ExitStack()
    with ctx:
        def sb(name, shape, dt=F32):
            return ctx.enter_context(nc.sbuf_tensor(name, shape, dt))

        def sem(name):
            return ctx.enter_context(nc.semaphore(name))

        x_sb = sb("x_sb", [C, TOK])
        c_sb = sb("c_sb", [C, B])
        vec = sb("vec", [C, NVEC])
        mask_sb = sb("mask_sb", [B, N], I32)
        scale_w = sb("scale_w", [C, C])
        shift_w = sb("shift_w", [C, C])
        qkv_w = sb("qkv_w", [C, 3 * C])
        proj_w = sb("proj_w", [C, C])
        w1 = sb("w1", [C, 2 * MLP])
        w2 = sb("w2", [C, MLP // C, C])
        mean_w = sb("mean_w", [C, C])
        ones = sb("ones", [B, C])
        ident = sb("ident", [C, C], BF16)
        eye8 = sb("eye8", [B, B])
        ones_row = sb("ones_row", [1, G * N], BF16)
        sig = sb("sig", [C, B])
        cond = sb("cond", [C, B])
        gain = sb("gain", [C, B])
        shift = sb("shift", [C, B])
        half_b1 = sb("half_b1", [C, MLP // C])
        valid = sb("valid", [B, N])
        any_valid = sb("any_valid", [B, 1])
        any_diag = sb("any_diag", [B, B])
        mask_add = sb("mask_add", [B, N], BF16)
        q_scale = sb("q_scale", [C, B])
        sq = sb("sq", [C, 2, CH])
        rs = sb("rs", [C, 2, CH])
        xn = sb("xn", [C, 2, CH])
        h = sb("h", [C, 2, CH])
        qk = sb("qk", [C, 2, 2, CH])
        rest = sb("rest", [C, 2, 2, CH])
        parts = sb("parts", [C, 2, 2, 3, CH], BF16)
        v_all = sb("v_all", [C, B, KT, H, VW])
        k_stack = sb("k_stack", [C, B, G, N], BF16)
        q_stack = [sb(f"q_stack{p}", [C, B, G, N], BF16) for p in range(2)]
        neg_max = sb("neg_max", [C, 2, G, KT])
        max_parts = sb("max_parts", [C, 2, KT, 2, G], BF16)
        max_rows = sb("max_rows", [2 * G, 2, N], BF16)
        p_exp = sb("p_exp", [C, 4, 2, KT, N])
        o_sb = sb("o_sb", [C, 2, CH])
        o_num = sb("o_num", [C, NC, CH])
        o_den = qk.rearrange("p c i t -> p (c i) t")
        y = rest.rearrange("p c i t -> p (c i) t")
        sq2, rs2 = sq, parts.rearrange("p c i j t -> p (c i j t)").bitcast(F32)[:, 0:NC * CH].rearrange("p (c t) -> p c t", c=NC)
        after_attention = p_exp.rearrange("p u r t q -> p (u r t q)").rearrange("p (s t) -> p s t", t=CH)
        h2 = after_attention[:, 0:NC, :]
        x1_half, th, silu = qk[:, 0, :, :], qk[:, 1, :, :], xn
        gated = after_attention[:, NC:NC + 3, :]
        out_sb = o_num

        bank = ctx.enter_context(nc.psum_tensor("bank", [C, 8, CH], F32))

        s_in = sem("s_in")
        s_x = [sem(f"s_x{c}") for c in range(NC)]
        s_wa = sem("s_wa")
        s_wb = sem("s_wb")
        s_const = sem("s_const")
        s_fill = sem("s_fill")
        s_sig = sem("s_sig")
        s_cond = sem("s_cond")
        s_small = sem("s_small")
        s_tab = sem("s_tab")
        s_sq = sem("s_sq")
        s_ss = sem("s_ss")
        s_rs = sem("s_rs")
        s_inv = sem("s_inv")
        s_inv2 = sem("s_inv2")
        s_rec = sem("s_rec")
        s_xn = sem("s_xn")
        s_h = sem("s_h")
        s_qk = sem("s_qk")
        s_v = sem("s_v")
        s_qk_out = sem("s_qk_out")
        s_v_out = sem("s_v_out")
        s_split = [sem("s_split_q"), sem("s_split_k")]
        s_pw = [sem(f"s_pw{i}") for i in range(2)]
        s_stack = [sem(f"s_stack{b}") for b in range(B)]
        s_zero = sem("s_zero")
        s_a = sem("s_a")
        s_ad = sem("s_ad")
        s_mp = sem("s_mp")
        s_mr = [sem(f"s_mr{i}") for i in range(2)]
        s_b = sem("s_b")
        s_e = sem("s_e")
        s_pv = sem("s_pv")
        s_od = sem("s_od")
        s_ow = [sem(f"s_ow{i}") for i in range(2)]
        s_or = [sem(f"s_or{c}") for c in range(NC)]
        s_on = sem("s_on")
        s_proj = sem("s_proj")
        s_y = sem("s_y")
        s_sq2 = sem("s_sq2")
        s_ss2 = sem("s_ss2")
        s_rs2 = sem("s_rs2")
        s_xn2 = sem("s_xn2")
        s_h2 = sem("s_h2")
        s_w1 = sem("s_w1")
        s_th = sem("s_th")
        s_silu = sem("s_silu")
        s_gated = sem("s_gated")
        s_w2 = sem("s_w2")
        s_out = sem("s_out")
        s_store = sem("s_store")

        block = ctx.enter_context(nc.Block())

        def stack_row(par, r):
            return 64 * par + r

        @block.sync
        def _(sp):
            sp.dma_start(c_sb[:, :], c_t).then_inc(s_in, 16)
            sp.dma_start(vec[:, :], vecs).then_inc(s_in, 16)
            sp.dma_start(mask_sb[:, :], mask).then_inc(s_in, 16)
            sp.dma_start(x_sb[:, 0:CH], x_t[:, 0:CH]).then_inc(s_x[0], 16)
            sp.dma_start(scale_w[:, :], scale_wt).then_inc(s_wa, 16)
            sp.dma_start(shift_w[:, :], shift_wt).then_inc(s_wa, 16)
            sp.dma_start(qkv_w[:, :], qkv_wt).then_inc(s_wa, 16)
            for c in range(1, NC):
                sp.dma_start(x_sb[:, c * CH:(c + 1) * CH], x_t[:, c * CH:(c + 1) * CH]).then_inc(s_x[c], 16)
            sp.dma_start(proj_w[:, :], proj_wt).then_inc(s_wb, 16)
            sp.dma_start(w1[:, :], w1_t).then_inc(s_wb, 16)
            sp.dma_start(w2[:, :, :], w2_t).then_inc(s_wb, 16)

            for c in range(NC):
                for i, (scratch, s) in enumerate(((q_parts, s_split[0]), (k_parts, s_split[1]))):
                    sp.wait_ge(s, 4 * (c + 1))
                    for j in range(3):
                        sp.dma_start(scratch[:, j, :, c * CH:(c + 1) * CH],
                                     parts[:, c % 2, i, j, :]).then_inc(s_pw[c % 2], 16)
                sp.wait_ge(s_pw[c % 2], 96 * (c // 2 + 1))
                if c == 0:
                    sp.wait_ge(s_tab, 6)
                for b in range(BC * c, BC * c + BC):
                    sp.wait_ge(s_fill, 3 * (b + 1))
                    for par in range(2):
                        for first, n in RUNS:
                            for stack, scratch, j in ((k_stack, k_parts, 3 - n), (q_stack[par], q_parts, 0)):
                                rows = scratch.rearrange("(g r) j d t -> r (j d) g t", r=2)
                                sp.dma_start(stack[stack_row(par, first):stack_row(par, first + n * D), b, :, :],
                                             rows[par, j * D:(j + n) * D, :, b * N:(b + 1) * N]).then_inc(s_stack[b], 16)
                        r = stack_row(par, ROW_MASK)
                        sp.dma_start(k_stack[r:r + 1, b, :, :],
                                     mask_add[b:b + 1, :].unsqueeze(1).to_broadcast([1, G, N])).then_inc(s_stack[b], 16)
                        sp.dma_start(q_stack[par][r:r + 1, b, :, :],
                                     ones_row[:, :].rearrange("a (g t) -> a g t", g=G)).then_inc(s_stack[b], 16)

            def rows_of_maxima(k):
                b, half = divmod(k, 2)
                sp.wait_ge(s_ad, turn_item(k) + 1)
                for j in range(2):
                    for par in range(2):
                        r = stack_row(par, ROW_MAX + j)
                        sp.dma_start(q_stack[par][r:r + 1, b, 4 * half:4 * half + 4, :],
                                     max_rows[8 * j + 4 * par:8 * j + 4 * par + 4, k % 2, :]).then_inc(s_mr[k % 2], 16)

            def store_rows(k):
                b, half = divmod(k, 2)
                sp.wait_ge(s_od, k + 1)
                for j in range(4):
                    dst = o_rows[b, 8 * half:8 * half + 8, :, :].rearrange("(q j) r t -> j r q t", j=4)
                    sp.dma_start(dst[j], o_sb[32 * j:32 * j + VW, k % 2, :].rearrange("r (q t) -> r q t", q=2))\
                      .then_inc(s_ow[k % 2], 16)

            def load_channels(b):
                for i in range(2):
                    sp.wait_ge(s_ow[i], 64 * (b + 1))
                c, at = divmod(b, BC)
                sp.dma_start(o_num[:, c, at * N:(at + 1) * N], o_rows[b, :, 0:D, :]).then_inc(s_or[c], 16)
                for i in range(H):
                    sp.dma_start(o_den[D * i:D * (i + 1), c, at * N:(at + 1) * N],
                                 o_rows[b, i, D:D + 1, :].to_broadcast([D, N])).then_inc(s_or[c], 16)

            rows_of_maxima(0)
            rows_of_maxima(1)
            for k in range(HALVES):
                if k + 2 < HALVES:
                    rows_of_maxima(k + 2)
                store_rows(k)
                if k % 2:
                    load_channels(k // 2)
            for c in range(NC):
                sp.wait_ge(s_out, c + 1)
                sp.dma_start(out_t[:, c * CH:(c + 1) * CH], out_sb[:, c, :]).then_inc(s_store, 16)
            sp.wait_ge(s_store, 16 * NC)

        @block.gpsimd
        def _(pool):
            nc.gpsimd.memset(mean_w[:, :], 1.0 / C).then_inc(s_const, 1)
            nc.gpsimd.memset(ident[:, :], 0.0).then_inc(s_const, 1)
            nc.gpsimd.memset(eye8[:, :], 0.0).then_inc(s_const, 1)
            pool.wait_ge(s_const, 3)
            nc.gpsimd.affine_select(out=eye8[:, :], in_=eye8[:, :], compare_op=ALU.not_equal, fill=1.0, base=0,
                                    pattern=[[-1, B]], channel_multiplier=1).then_inc(s_const, 1)
            nc.gpsimd.affine_select(out=ident[:, :], in_=ident[:, :], compare_op=ALU.not_equal, fill=1.0, base=0,
                                    pattern=[[-1, C]], channel_multiplier=1).then_inc(s_const, 1)
            nc.gpsimd.memset(ones[:, :], 1.0).then_inc(s_const, 1)
            nc.gpsimd.memset(ones_row[:, :], 1.0).then_inc(s_const, 1)
            nc.gpsimd.memset(v_all[:, :, :, :, D:VW], 1.0).then_inc(s_const, 1)

            def fill(b):
                words = [t[:, b, :, :].rearrange("p g t -> p (g t)").bitcast(U32) for t in (k_stack, *q_stack)]
                nc.gpsimd.memset(words[0], ONES_BF16).then_inc(s_fill, 1)
                nc.gpsimd.memset(words[1], 0).then_inc(s_fill, 1)
                nc.gpsimd.memset(words[2], 0).then_inc(s_fill, 1)

            fill(0)
            for c in range(NC):
                for b in range(BC * c, BC * c + BC):
                    at = (b % BC) * N
                    pool.wait_ge(s_xn, b + 1)
                    if c >= 2:
                        pool.wait_ge(s_v, c - 1)
                    nc.gpsimd.tensor_scalar(h[:, c % 2, at:at + N], xn[:, c % 2, at:at + N], shift[:, b:b + 1], None,
                                            ALU.add).then_inc(s_h, 1)
                for b in range(BC * c + 1, min(BC * c + 1 + BC, B)):
                    fill(b)
            for k in range(HALVES):
                pool.wait_ge(s_ad, unit_item(4 * k + 3) + 2)
                if k >= 2:
                    pool.wait_ge(s_a, turn_item(k - 2) + 1)
                neg = neg_max[:, k % 2, :, :].rearrange("p g q -> p q g")
                nc.gpsimd.tensor_copy(max_parts[:, k % 2, :, 0, :], neg).then_inc(s_mp, 1)
                pool.wait_ge(s_mp, 2 * k + 1)
                nc.gpsimd.tensor_tensor(max_parts[:, k % 2, :, 1, :], neg, max_parts[:, k % 2, :, 0, :],
                                        ALU.subtract).then_inc(s_mp, 1)
            for c in range(NC):
                for b in range(BC * c, BC * c + BC):
                    at = (b % BC) * N
                    pool.wait_ge(s_xn2, b + 1)
                    nc.gpsimd.tensor_scalar(h2[:, c, at:at + N], h2[:, c, at:at + N], shift[:, b:b + 1], None,
                                            ALU.add).then_inc(s_h2, 1)

        @block.tensor
        def _(pe):
            pe.wait_ge(s_wa, 48)
            pe.wait_ge(s_cond, 2)
            nc.tensor.matmul(bank[:, 0, 0:B], scale_w[:, :], cond[:, :], start=True, stop=True)
            nc.tensor.matmul(bank[:, 1, 0:B], shift_w[:, :], cond[:, :], start=True, stop=True).then_inc(s_small, 1)
            pe.wait_ge(s_const, 6)
            pe.wait_ge(s_tab, 5)
            nc.tensor.matmul(bank[:, 2, 0:B], ones[:, :], any_diag[:, :], start=True, stop=True).then_inc(s_small, 1)

            def mean_square(c):
                pe.wait_ge(s_sq, c + 1)
                if c >= 2:
                    pe.wait_ge(s_rs, c - 1)
                nc.tensor.matmul(bank[:, 3 + c % 2, :], mean_w[:, :], sq[:, c % 2, :],
                                 start=True, stop=True).then_inc(s_ss, 1)

            mean_square(0)
            for c in range(NC):
                if c + 1 < NC:
                    mean_square(c + 1)
                pe.wait_ge(s_h, BC * (c + 1))
                for i in range(2):
                    if c >= 1:
                        pe.wait_ge(s_qk_out, 3 * (c - 1) + (2, 3)[i])
                    nc.tensor.matmul(bank[:, 5 + i, :], qkv_w[:, i * C:(i + 1) * C], h[:, c % 2, :],
                                     start=True, stop=True).then_inc(s_qk, 1)
                if c >= 1:
                    pe.wait_ge(s_v_out, c)
                for t in range(CH // C):
                    mm = nc.tensor.matmul(bank[:, 7, t * C:(t + 1) * C], h[:, c % 2, t * C:(t + 1) * C],
                                          qkv_w[:, 2 * C:3 * C], start=True, stop=True)
                mm.then_inc(s_v, 1)

            def query_scores(u):
                b, g = divmod(u, G)
                if g == 0:
                    pe.wait_ge(s_stack[b], 16 * 16)
                for par in range(2):
                    n = unit_item(u) + par
                    if n >= 2:
                        pe.wait_ge(s_ad, n - 1)
                    for t in range(KT):
                        mm = nc.tensor.matmul(bank[:, n % 2, t * N:(t + 1) * N],
                                              q_stack[par][:, b, g, t * 128:(t + 1) * 128], k_stack[:, b, g, :],
                                              start=True, stop=True)
                    mm.then_inc(s_a, 1)

            def turn_maxima(k):
                n = turn_item(k)
                pe.wait_ge(s_ad, n - 1)
                pe.wait_ge(s_mp, 2 * (k + 1))
                for t in range(KT):
                    mm = nc.tensor.transpose(bank[0:2 * G, n % 2, t * 64:(t + 1) * 64].bitcast(BF16),
                                             max_parts[:, k % 2, t, :, :].rearrange("p j g -> p (j g)"), ident[:, :])
                mm.then_inc(s_a, 1)

            def key_scores(u):
                b, g = divmod(u, G)
                if g % 4 == 0:
                    k = u // 4
                    pe.wait_ge(s_mr[k % 2], 64 * (k // 2 + 1))
                if u >= 2:
                    pe.wait_ge(s_e, u - 1)
                for t in range(KT):
                    for par in range(2):
                        mm = nc.tensor.matmul(bank[:, 2 + 2 * (u % 2) + par, t * N:(t + 1) * N],
                                              k_stack[:, b, g, t * 128:(t + 1) * 128], q_stack[par][:, b, g, :],
                                              start=True, stop=True)
                mm.then_inc(s_b, 1)

            def p_times_v(q):
                b, g = divmod(2 * q, G)
                k = q // 2
                pe.wait_ge(s_e, 2 * q + 2)
                if q == 0:
                    pe.wait_ge(s_zero, 1)
                if q % 2 == 0 and k >= 2:
                    pe.wait_ge(s_od, k - 1)
                for t in range(KT):
                    for j in range(4):
                        mm = nc.tensor.matmul(bank[32 * j:32 * j + VW, 6 + k % 2, (q % 2) * N:(q % 2 + 1) * N],
                                              v_all[:, b, t, 2 * g + j, :],
                                              p_exp[:, (2 * q + j // 2) % 4, j % 2, t, :],
                                              start=(t == 0), stop=(t == KT - 1), tile_position=(0, 32 * j))
                mm.then_inc(s_pv, 1)

            for u in range(G):
                query_scores(u)
                if u == 4:
                    turn_maxima(0)
            pe.wait_ge(s_const, 8)
            pe.wait_ge(s_v_out, NC)
            for u in range(UNITS):
                if u + G < UNITS:
                    query_scores(u + G)
                if u % 4 == 0 and u < UNITS - 4:
                    turn_maxima(u // 4 + 1)
                key_scores(u)
                if u % 2 == 0 and u >= 2:
                    p_times_v(u // 2 - 1)
            p_times_v(UNITS // 2 - 1)

            pe.wait_ge(s_wb, 48)
            for c in range(NC):
                pe.wait_ge(s_on, c + 1)
                nc.tensor.matmul(bank[:, c, :], proj_w[:, :], o_num[:, c, :], start=True, stop=True).then_inc(s_proj, 1)
            for c in range(NC):
                pe.wait_ge(s_sq2, c + 1)
                nc.tensor.matmul(bank[:, 4 + c, :], mean_w[:, :], sq2[:, c % 2, :],
                                 start=True, stop=True).then_inc(s_ss2, 1)

            def mlp_out(n):
                c, m = divmod(n, MLP // C)
                pe.wait_ge(s_gated, n + 1)
                if m == 0 and c >= 2:
                    pe.wait_ge(s_out, c - 1)
                mm = nc.tensor.matmul(bank[:, 6 + c % 2, :], w2[:, m, :], gated[:, n % 3, :],
                                      start=(m == 0), stop=(m == MLP // C - 1))
                if m == MLP // C - 1:
                    mm.then_inc(s_w2, 1)

            pe.wait_ge(s_rs2, NC)
            for n in range(NC * MLP // C):
                c, m = divmod(n, MLP // C)
                if m == 0:
                    pe.wait_ge(s_h2, BC * (c + 1))
                if n >= 3:
                    pe.wait_ge(s_gated, n - 2)
                nc.tensor.matmul(bank[:, 2 * (n % 3), :], w1[:, m * C:(m + 1) * C], h2[:, c, :],
                                 start=True, stop=True).then_inc(s_w1, 1)
                nc.tensor.matmul(bank[:, 2 * (n % 3) + 1, :], w1[:, MLP + m * C:MLP + (m + 1) * C], h2[:, c, :],
                                 start=True, stop=True).then_inc(s_w1, 1)
                if n >= 1:
                    mlp_out(n - 1)
            mlp_out(NC * MLP // C - 1)

        @block.scalar
        def _(act):
            act.wait_ge(s_in, 48)
            nc.scalar.activation(sig[:, :], c_sb[:, :], ACT.Exp, scale=-1.0).then_inc(s_sig, 1)

            def square(c):
                act.wait_ge(s_x[c], 16)
                if c >= 2:
                    act.wait_ge(s_ss, c - 1)
                nc.scalar.activation(sq[:, c % 2, :], x_sb[:, c * CH:(c + 1) * CH], ACT.Square).then_inc(s_sq, 1)

            def power(t, exponent, s, n):
                nc.scalar.activation(t, t, ACT.Ln).then_inc(s, 1)
                act.wait_ge(s, n)
                nc.scalar.activation(t, t, ACT.Exp, scale=exponent).then_inc(s, 1)

            def inverse_norm(c):
                act.wait_ge(s_rs, c + 1)
                power(rs[:, c % 2, :], -0.5, s_inv, 2 * c + 1)

            square(0)
            square(1)
            inverse_norm(0)
            inverse_norm(1)
            act.wait_ge(s_tab, 7)
            for c in range(NC):
                act.wait_ge(s_qk, 2 * c + 1)
                if c >= 2:
                    act.wait_ge(s_split[0], 4 * (c - 1))
                for i in range(BC):
                    nc.scalar.activation(qk[:, c % 2, 0, i * N:(i + 1) * N], bank[:, 5, i * N:(i + 1) * N], ACT.Copy,
                                         scale=q_scale[:, BC * c + i:BC * c + i + 1]).then_inc(s_qk_out, 1)
                act.wait_ge(s_qk, 2 * c + 2)
                if c >= 2:
                    act.wait_ge(s_split[1], 4 * (c - 1))
                nc.scalar.activation(qk[:, c % 2, 1, :], bank[:, 6, :], ACT.Copy).then_inc(s_qk_out, 1)
                act.wait_ge(s_v, c + 1)
                nc.scalar.activation(v_all[:, BC * c:BC * (c + 1), :, :, 0:D],
                                     bank[:, 7, :].rearrange("p (b t h d) -> p b t h d", b=BC, t=KT, h=H),
                                     ACT.Copy).then_inc(s_v_out, 1)
                if c + 2 < NC:
                    square(c + 2)
                    inverse_norm(c + 2)

            def drain_output(k):
                act.wait_ge(s_pv, 2 * k + 2)
                if k >= 2:
                    act.wait_ge(s_ow[k % 2], 64 * (k // 2))
                nc.scalar.activation(o_sb[:, k % 2, :], bank[:, 6 + k % 2, :], ACT.Copy).then_inc(s_od, 1)

            def inverse_sum(c):
                act.wait_ge(s_or[c], 16 * BC * (H + 1))
                power(o_den[:, c, :], -1.0, s_rec, 2 * c + 1)

            for u in range(UNITS):
                act.wait_ge(s_b, u + 1)
                if u >= 4:
                    act.wait_ge(s_pv, u // 2 - 1)
                nc.scalar.activation(p_exp[:, u % 4, :, :, :],
                                     bank[:, 2 + 2 * (u % 2):4 + 2 * (u % 2), :].rearrange("p r (t q) -> p r t q", t=KT),
                                     ACT.Exp).then_inc(s_e, 1)
                if u % 4 == 1 and u >= 5:
                    drain_output(u // 4 - 1)
                if u % 16 == 12 and u >= 16:
                    inverse_sum(u // 16 - 1)
            drain_output(HALVES - 1)
            inverse_sum(NC - 1)

            for c in range(NC):
                act.wait_ge(s_y, c + 1)
                if c >= 2:
                    act.wait_ge(s_ss2, c - 1)
                nc.scalar.activation(sq2[:, c % 2, :], y[:, c, :], ACT.Square).then_inc(s_sq2, 1)
            for c in range(NC):
                act.wait_ge(s_rs2, c + 1)
                power(rs2[:, c, :], -0.5, s_inv2, 2 * c + 1)
            for n in range(NC * MLP // C):
                m = n % (MLP // C)
                act.wait_ge(s_w1, 2 * n + 1)
                if n >= 2:
                    act.wait_ge(s_silu, n - 1)
                nc.scalar.activation(x1_half[:, n % 2, :], bank[:, 2 * (n % 3), :], ACT.Identity,
                                     bias=half_b1[:, m:m + 1], scale=0.5).then_inc(s_th, 1)
                nc.scalar.activation(th[:, n % 2, :], bank[:, 2 * (n % 3), :], ACT.Tanh,
                                     bias=half_b1[:, m:m + 1], scale=0.5).then_inc(s_th, 1)

        @block.vector
        def _(dve):
            dve.wait_ge(s_in, 48)
            nc.vector.tensor_scalar(half_b1[:, :], vec[:, V_B1:V_B1 + MLP // C], 0.5, None, ALU.mult).then_inc(s_tab, 1)
            nc.vector.tensor_scalar(valid[:, :], mask_sb[:, :], 0.0, None, ALU.not_equal).then_inc(s_tab, 1)
            dve.wait_ge(s_sig, 1)
            nc.vector.tensor_scalar(sig[:, :], sig[:, :], 1.0, None, ALU.add).then_inc(s_tab, 1)
            dve.wait_ge(s_tab, 3)
            nc.vector.tensor_reduce(out=any_valid[:, :], in_=valid[:, :], axis=AX.X, op=ALU.max).then_inc(s_tab, 1)
            dve.wait_ge(s_tab, 4)
            nc.vector.reciprocal(sig[:, :], sig[:, :]).then_inc(s_cond, 1)
            dve.wait_ge(s_cond, 1)
            nc.vector.tensor_tensor(cond[:, :], c_sb[:, :], sig[:, :], ALU.mult).then_inc(s_cond, 1)
            dve.wait_ge(s_const, 5)
            nc.vector.tensor_scalar(any_diag[:, :], eye8[:, :], any_valid[:, :], None, ALU.mult).then_inc(s_tab, 1)
            nc.vector.tensor_scalar(valid[:, :], valid[:, :], 1.0, -MASKED, ALU.subtract, ALU.mult).then_inc(s_cond, 1)
            dve.wait_ge(s_cond, 3)
            nc.vector.tensor_scalar(mask_add[:, :], valid[:, :], any_valid[:, :], None, ALU.mult).then_inc(s_tab, 1)
            dve.wait_ge(s_small, 2)
            nc.vector.tensor_scalar(q_scale[:, :], bank[:, 2, 0:B], D ** -0.5, None, ALU.mult).then_inc(s_tab, 1)
            nc.vector.tensor_scalar(shift[:, :], bank[:, 1, 0:B], vec[:, V_SHIFT_B:V_SHIFT_B + 1], None,
                                    ALU.add).then_inc(s_tab, 1)
            nc.vector.tensor_scalar(gain[:, :], bank[:, 0, 0:B], vec[:, V_SCALE_B:V_SCALE_B + 1], 1.0,
                                    ALU.add, ALU.add).then_inc(s_tab, 1)
            dve.wait_ge(s_tab, 9)
            nc.vector.tensor_scalar(gain[:, :], gain[:, :], 0.1, 10.0, ALU.max, ALU.min).then_inc(s_tab, 1)
            dve.wait_ge(s_tab, 10)
            nc.vector.tensor_scalar(gain[:, :], gain[:, :], vec[:, V_NORM:V_NORM + 1], None, ALU.mult).then_inc(s_tab, 1)
            dve.wait_ge(s_tab, 11)

            def guard(c):
                dve.wait_ge(s_ss, c + 1)
                nc.vector.tensor_scalar(rs[:, c % 2, :], bank[:, 3 + c % 2, :], EPS * EPS, None,
                                        ALU.max).then_inc(s_rs, 1)

            def norm(c):
                dve.wait_ge(s_inv, 2 * c + 2)
                for i in range(BC):
                    b = BC * c + i
                    if c >= 2:
                        dve.wait_ge(s_h, b - 3)
                    nc.vector.scalar_tensor_tensor(out=xn[:, c % 2, i * N:(i + 1) * N],
                                                   in0=x_sb[:, b * N:(b + 1) * N], scalar=gain[:, b:b + 1],
                                                   in1=rs[:, c % 2, i * N:(i + 1) * N],
                                                   op0=ALU.mult, op1=ALU.mult).then_inc(s_xn, 1)

            def split(c, i):
                dve.wait_ge(s_qk_out, 3 * c + 2 + i)
                if c >= 2:
                    dve.wait_ge(s_pw[c % 2], 96 * (c // 2))
                src, r = qk[:, c % 2, i, :], rest[:, c % 2, i, :]
                part = [parts[:, c % 2, i, (2 - j if i else j), :] for j in range(3)]
                s, done = s_split[i], 4 * c
                nc.vector.tensor_copy(part[0], src).then_inc(s, 1)
                dve.wait_ge(s, done + 1)
                nc.vector.tensor_tensor(r, src, part[0], ALU.subtract).then_inc(s, 1)
                dve.wait_ge(s, done + 2)
                nc.vector.tensor_copy(part[1], r).then_inc(s, 1)
                dve.wait_ge(s, done + 3)
                nc.vector.tensor_tensor(part[2], r, part[1], ALU.subtract).then_inc(s, 1)

            guard(0)
            guard(1)
            norm(0)
            for c in range(NC):
                if c + 1 < NC:
                    norm(c + 1)
                if c + 2 < NC:
                    guard(c + 2)
                for i in range(2):
                    split(c, i)
            dve.wait_ge(s_qk_out, 3 * NC)
            dve.wait_ge(s_v_out, NC)
            nc.vector.memset(bank[:, 6:8, :], 0.0).then_inc(s_zero, 1)

            def maxima(u):
                k, g = divmod(u, 4)
                if g == 0 and k >= 2:
                    dve.wait_ge(s_mp, 2 * (k - 1))
                for par in range(2):
                    n = unit_item(u) + par
                    dve.wait_ge(s_a, n + 1)
                    nc.vector.tensor_reduce(out=neg_max[:, k % 2, 4 * par + g, :],
                                            in_=bank[:, n % 2, :].rearrange("p (t k) -> p t k", t=KT),
                                            axis=AX.X, op=ALU.max, negate=True).then_inc(s_ad, 1)

            def turned(k):
                n = turn_item(k)
                dve.wait_ge(s_a, n + 1)
                if k >= 2:
                    dve.wait_ge(s_mr[k % 2], 64 * (k // 2))
                nc.vector.tensor_copy(max_rows[:, k % 2, :],
                                      bank[0:2 * G, n % 2, 0:2 * 64].bitcast(BF16)).then_inc(s_ad, 1)

            for u in range(UNITS):
                maxima(u)
                if u % 4 == 0 and u >= 4:
                    turned(u // 4 - 1)
            turned(HALVES - 1)

            for c in range(NC):
                dve.wait_ge(s_rec, 2 * c + 2)
                nc.vector.tensor_tensor(o_num[:, c, :], o_num[:, c, :], o_den[:, c, :], ALU.mult).then_inc(s_on, 1)
            for c in range(NC):
                dve.wait_ge(s_proj, c + 1)
                nc.vector.scalar_tensor_tensor(out=y[:, c, :], in0=bank[:, c, :], scalar=vec[:, V_PROJ_B:V_PROJ_B + 1],
                                               in1=x_sb[:, c * CH:(c + 1) * CH], op0=ALU.add, op1=ALU.add).then_inc(s_y, 1)
            for c in range(NC):
                dve.wait_ge(s_ss2, c + 1)
                nc.vector.tensor_scalar(rs2[:, c, :], bank[:, 4 + c, :], EPS * EPS, None, ALU.max).then_inc(s_rs2, 1)
            for c in range(NC):
                dve.wait_ge(s_inv2, 2 * c + 2)
                for i in range(BC):
                    b = BC * c + i
                    nc.vector.scalar_tensor_tensor(out=h2[:, c, i * N:(i + 1) * N],
                                                   in0=y[:, c, i * N:(i + 1) * N], scalar=gain[:, b:b + 1],
                                                   in1=rs2[:, c, i * N:(i + 1) * N],
                                                   op0=ALU.mult, op1=ALU.mult).then_inc(s_xn2, 1)

            def add_out(c):
                dve.wait_ge(s_w2, c + 1)
                nc.vector.scalar_tensor_tensor(out=out_sb[:, c, :], in0=bank[:, 6 + c % 2, :],
                                               scalar=vec[:, V_B2:V_B2 + 1], in1=y[:, c, :],
                                               op0=ALU.add, op1=ALU.add).then_inc(s_out, 1)

            for n in range(NC * MLP // C):
                c, m = divmod(n, MLP // C)
                dve.wait_ge(s_th, 2 * n + 2)
                nc.vector.scalar_tensor_tensor(out=silu[:, n % 2, :], in0=th[:, n % 2, :], scalar=1.0,
                                               in1=x1_half[:, n % 2, :], op0=ALU.add, op1=ALU.mult).then_inc(s_silu, 1)
                dve.wait_ge(s_silu, n + 1)
                dve.wait_ge(s_w1, 2 * n + 2)
                b1 = vec[:, V_B1 + MLP // C + m:V_B1 + MLP // C + m + 1]
                nc.vector.scalar_tensor_tensor(out=gated[:, n % 3, :], in0=bank[:, 2 * (n % 3) + 1, :], scalar=b1,
                                               in1=silu[:, n % 2, :], op0=ALU.add, op1=ALU.mult).then_inc(s_gated, 1)
                if m == 0 and c >= 1:
                    add_out(c - 1)
            add_out(NC - 1)


def kernel(x, cond_1024, mask_BxS_ik0, L0_cond_norm_w, L0_cond_scale_w, L0_cond_scale_b, L0_cond_shift_w,
           L0_cond_shift_b, L0_cond_qkv_w, L0_cond_proj_w, L0_cond_proj_b, L0_cond_mlp_w1, L0_cond_mlp_b1,
           L0_cond_mlp_w2, L0_cond_mlp_b2):
    import numpy as np
    import concourse.bacc as bacc
    from concourse.bass_utils import run_bass_kernel_spmd

    def turned(a):
        return np.ascontiguousarray(np.asarray(a).T)

    vectors = [np.asarray(v).reshape(-1, C) for v in
               (L0_cond_norm_w, L0_cond_scale_b, L0_cond_shift_b, L0_cond_proj_b, L0_cond_mlp_b2, L0_cond_mlp_b1)]
    w2 = np.asarray(L0_cond_mlp_w2).T.reshape(MLP // C, C, C).transpose(1, 0, 2)
    arrays = {
        "x_t": turned(np.asarray(x).reshape(TOK, C)),
        "c_t": turned(cond_1024),
        "mask": np.ascontiguousarray(mask_BxS_ik0),
        "vecs": turned(np.concatenate(vectors, axis=0)),
        "scale_wt": turned(L0_cond_scale_w),
        "shift_wt": turned(L0_cond_shift_w),
        "qkv_wt": turned(L0_cond_qkv_w),
        "proj_wt": turned(L0_cond_proj_w),
        "w1_t": turned(L0_cond_mlp_w1),
        "w2_t": np.ascontiguousarray(w2),
    }
    nc = bacc.Bacc("TRN2", target_bir_lowering=False, num_devices=1)
    args = [nc.dram_tensor(name, a.shape, mybir.dt.from_np(a.dtype), kind="ExternalInput").ap()
            for name, a in arrays.items()]
    out_t = nc.dram_tensor("out_t", (C, TOK), F32, kind="ExternalOutput").ap()
    build(nc, *args, out_t)
    result = run_bass_kernel_spmd(nc, [arrays], core_ids=[0]).results[0]["out_t"]
    return np.ascontiguousarray(result.T).reshape(B, N, C)
```

```python
from contextlib import ExitStack

import concourse.bass as bass
from concourse import mybir

F32 = mybir.dt.float32
BF16 = mybir.dt.bfloat16
I32 = mybir.dt.int32
U32 = mybir.dt.uint32
ALU = mybir.AluOpType
ACT = mybir.ActivationFunctionType
AX = mybir.AxisListType

C = 128
B, N = 8, 256
TOK = B * N
H, D = 16, 8
MLP = 4 * C
G = H // 2
CH = 512
NC = TOK // CH
BC = CH // N
KT = N // 128
VW = D + 1
EPS = 1e-6
MASKED = -float(2 ** 100)
ONES_BF16 = 0x3F803F80

Q_PARTS = [0, 0, 0, 1, 1, 2]
K_PARTS = [0, 1, 2, 0, 1, 0]
SLOTS = len(Q_PARTS)
HEAD_ROWS = D * SLOTS
ROW_MASK = 2 * HEAD_ROWS
ROW_MAX = ROW_MASK + 1
HALVES = 2 * B
UNITS = B * G

MT = MLP // C
RING = 3
LAG = 2
LATE = 4

V_NORM, V_SCALE_B, V_SHIFT_B, V_PROJ_B, V_B2, V_B1 = 0, 1, 2, 3, 4, 5
NVEC = V_B1 + 2 * MLP // C


def unit_item(u):
    return 2 * u + (max(u, 1) - 1) // 4


def turn_item(k):
    return min(2 * (4 * k + 5), 2 * UNITS) + k


def build(nc, x_t, c_t, mask, vecs, scale_wt, shift_wt, qkv_wt, proj_wt, w1_t, w2_t, out_t):
    q_rows = nc.dram_tensor("q_rows", [C, SLOTS, TOK], BF16).ap()
    k_rows = nc.dram_tensor("k_rows", [C, SLOTS, TOK], BF16).ap()
    o_rows = nc.dram_tensor("o_rows", [B, H, 32, N], F32).ap()

    ctx = ExitStack()
    with ctx:
        def sb(name, shape, dt=F32):
            return ctx.enter_context(nc.sbuf_tensor(name, shape, dt))

        def sem(name):
            return ctx.enter_context(nc.semaphore(name))

        x_sb = sb("x_sb", [C, TOK])
        c_sb = sb("c_sb", [C, B])
        vec = sb("vec", [C, NVEC])
        mask_sb = sb("mask_sb", [B, N], I32)
        scale_w = sb("scale_w", [C, C])
        shift_w = sb("shift_w", [C, C])
        qkv_w = sb("qkv_w", [C, 3 * C])
        proj_w = sb("proj_w", [C, C])
        w1 = sb("w1", [C, 2 * MLP])
        w2 = sb("w2", [C, MT, C])
        mean_w = sb("mean_w", [C, C])
        ones = sb("ones", [B, C])
        ident = sb("ident", [C, C], BF16)
        eye8 = sb("eye8", [B, B])
        ones_row = sb("ones_row", [1, CH], BF16)
        sig = sb("sig", [C, B])
        cond = sb("cond", [C, B])
        gain = sb("gain", [C, B])
        shift = sb("shift", [C, B])
        half_b1 = sb("half_b1", [C, MT])
        valid = sb("valid", [B, N])
        any_valid = sb("any_valid", [B, 1])
        any_diag = sb("any_diag", [B, B])
        mask_add = sb("mask_add", [B, N], BF16)
        any_all = sb("any_all", [C, B])
        sq = sb("sq", [C, 2, CH])
        rs = sb("rs", [C, NC, CH])
        xn = sb("xn", [C, 2, CH])
        h = sb("h", [C, 2, CH])
        o_den = sb("o_den", [C, NC, CH])
        rest = sb("rest", [C, 2, 2, CH])
        parts = sb("parts", [C, 2, 2, 3, CH], BF16)
        v_all = sb("v_all", [C, B, KT, H, VW])
        k_stack = sb("k_stack", [C, NC, G, CH], BF16)
        q_stack = [sb(f"q_stack{p}", [C, NC, G, CH], BF16) for p in range(2)]
        neg_max = sb("neg_max", [C, 2, KT, 2, G // 2])
        max_parts = sb("max_parts", [C, 2, KT, 2, 2, G // 2], BF16)
        max_rows = sb("max_rows", [2 * G, 2, N], BF16)
        p_exp = sb("p_exp", [C, 4, 2, KT, N])
        o_sb = sb("o_sb", [C, 2, CH])
        o_num = sb("o_num", [C, NC, CH])
        y = rest.rearrange("p c i t -> p (c i) t")
        sq2, rs2 = sq, parts.rearrange("p c i j t -> p (c i j t)").bitcast(F32)[:, 0:NC * CH].rearrange("p (c t) -> p c t", c=NC)
        free = k_stack[:, 0:NC - 1, :, :].rearrange("p c g t -> p (c g t)").bitcast(F32)\
                                         .rearrange("p (s t) -> p s t", t=CH)
        xn2 = h2 = free[:, 0:NC, :]
        x1_half, th, gated, silu = free[:, 4:6, :], free[:, 6:8, :], free[:, 8:11, :], xn
        out_sb = o_num

        bank = ctx.enter_context(nc.psum_tensor("bank", [C, 8, CH], F32))

        s_in = sem("s_in")
        s_x = [sem(f"s_x{c}") for c in range(NC)]
        s_wa = sem("s_wa")
        s_wb = sem("s_wb")
        s_const = sem("s_const")
        s_fill = sem("s_fill")
        s_sig = sem("s_sig")
        s_cond = sem("s_cond")
        s_small = sem("s_small")
        s_tab = sem("s_tab")
        s_sq = sem("s_sq")
        s_ss = sem("s_ss")
        s_rs = sem("s_rs")
        s_inv = sem("s_inv")
        s_inv2 = sem("s_inv2")
        s_rec = sem("s_rec")
        s_xn = sem("s_xn")
        s_h = sem("s_h")
        s_qk = sem("s_qk")
        s_v = sem("s_v")
        s_part0 = [sem("s_part0_q"), sem("s_part0_k")]
        s_rest = [sem("s_rest_q"), sem("s_rest_k")]
        s_v_out = sem("s_v_out")
        s_split = [sem("s_split_q"), sem("s_split_k")]
        s_pw = [sem(f"s_pw{i}") for i in range(2)]
        s_stack = [sem(f"s_stack{c}") for c in range(NC)]
        s_zero = sem("s_zero")
        s_a = sem("s_a")
        s_ad = sem("s_ad")
        s_mp = sem("s_mp")
        s_mr = [sem(f"s_mr{i}") for i in range(2)]
        s_b = sem("s_b")
        s_e = sem("s_e")
        s_pv = sem("s_pv")
        s_od = sem("s_od")
        s_ow = [sem(f"s_ow{i}") for i in range(2)]
        s_or = [sem(f"s_or{c}") for c in range(NC)]
        s_on = sem("s_on")
        s_proj = sem("s_proj")
        s_y = sem("s_y")
        s_sq2 = sem("s_sq2")
        s_ss2 = sem("s_ss2")
        s_rs2 = sem("s_rs2")
        s_xn2 = sem("s_xn2")
        s_h2 = sem("s_h2")
        s_w1 = sem("s_w1")
        s_th = sem("s_th")
        s_silu = sem("s_silu")
        s_gated = sem("s_gated")
        s_w2 = sem("s_w2")
        s_out = sem("s_out")
        s_store = sem("s_store")

        block = ctx.enter_context(nc.Block())

        @block.sync
        def _(sp):
            sp.dma_start(x_sb[:, 0:CH], x_t[:, 0:CH]).then_inc(s_x[0], 16)
            sp.dma_start(c_sb[:, :], c_t).then_inc(s_in, 16)
            sp.dma_start(vec[:, :], vecs).then_inc(s_in, 16)
            sp.dma_start(mask_sb[:, :], mask).then_inc(s_in, 16)
            sp.dma_start(x_sb[:, CH:2 * CH], x_t[:, CH:2 * CH]).then_inc(s_x[1], 16)
            sp.dma_start(scale_w[:, :], scale_wt).then_inc(s_wa, 16)
            sp.dma_start(shift_w[:, :], shift_wt).then_inc(s_wa, 16)
            sp.dma_start(qkv_w[:, :], qkv_wt).then_inc(s_wa, 16)
            for c in range(2, NC):
                sp.dma_start(x_sb[:, c * CH:(c + 1) * CH], x_t[:, c * CH:(c + 1) * CH]).then_inc(s_x[c], 16)
            sp.dma_start(proj_w[:, :], proj_wt).then_inc(s_wb, 16)
            sp.dma_start(w1[:, :], w1_t).then_inc(s_wb, 16)
            sp.dma_start(w2[:, :, :], w2_t).then_inc(s_wb, 16)

            for c in range(NC):
                tok = slice(c * CH, (c + 1) * CH)
                if c == 0:
                    sp.wait_ge(s_tab, 6)
                sp.wait_ge(s_fill, 3 * (c + 1))
                for i in range(BC):
                    b = BC * c + i
                    sp.dma_start(k_stack[ROW_MASK:ROW_MASK + 1, c, :, i * N:(i + 1) * N],
                                 mask_add[b:b + 1, :].unsqueeze(1).to_broadcast([1, G, N])).then_inc(s_stack[c], 16)
                for par in range(2):
                    sp.dma_start(q_stack[par][ROW_MASK:ROW_MASK + 1, c, :, :],
                                 ones_row[:, :].unsqueeze(1).to_broadcast([1, G, CH])).then_inc(s_stack[c], 16)
                for j in range(3):
                    sp.wait_ge(*((s_part0[0], BC * (c + 1)), (s_split[0], 2 * c + 1), (s_split[0], 2 * c + 2))[j])
                    n, first = 3 - j, Q_PARTS.index(j)
                    sp.dma_start(q_rows[:, first:first + n, tok],
                                 parts[:, c % 2, 0, j:j + 1, :].to_broadcast([C, n, CH])).then_inc(s_pw[c % 2], 16)
                sp.wait_ge(s_split[1], 2 * (c + 1))
                for n, first in ((3, 0), (2, 3), (1, 5)):
                    sp.dma_start(k_rows[:, first:first + n, tok], parts[:, c % 2, 1, 0:n, :]).then_inc(s_pw[c % 2], 16)
                sp.wait_ge(s_pw[c % 2], 96 * (c // 2 + 1))
                for par in range(2):
                    rows = q_rows[:, :, tok].rearrange("(g r d) s t -> r (d s) g t", r=2, d=D)
                    sp.dma_start(q_stack[par][par * HEAD_ROWS:(par + 1) * HEAD_ROWS, c, :, :],
                                 rows[par]).then_inc(s_stack[c], 16)
                sp.dma_start(k_stack[0:2 * HEAD_ROWS, c, :, :],
                             k_rows[:, :, tok].rearrange("(g e) s t -> (e s) g t", e=2 * D)).then_inc(s_stack[c], 16)

            for k in range(HALVES):
                b, half = divmod(k, 2)
                sp.wait_ge(s_od, k + 1)
                dst = o_rows[b, 8 * half:8 * half + 8, :, :].rearrange("(q j) r t -> (j r) q t", j=4)
                sp.dma_start(dst, o_sb[:, k % 2, :].rearrange("r (q t) -> r q t", q=2)).then_inc(s_ow[k % 2], 16)
                if half:
                    for i in range(2):
                        sp.wait_ge(s_ow[i], 16 * (b + 1))
                    c, at = divmod(b, BC)
                    sp.dma_start(o_num[:, c, at * N:(at + 1) * N], o_rows[b, :, 0:D, :]).then_inc(s_or[c], 16)
                    sp.dma_start(o_den[:, c, at * N:(at + 1) * N],
                                 o_rows[b, :, D:D + 1, :].to_broadcast([H, D, N])).then_inc(s_or[c], 16)
            for c in range(NC):
                sp.wait_ge(s_out, c + 1)
                sp.dma_start(out_t[:, c * CH:(c + 1) * CH], out_sb[:, c, :]).then_inc(s_store, 16)
            sp.wait_ge(s_store, 16 * NC)

        @block.gpsimd
        def _(pool):
            nc.gpsimd.memset(mean_w[:, :], 1.0 / C).then_inc(s_const, 1)
            nc.gpsimd.memset(ident[:, :], 0.0).then_inc(s_const, 1)
            nc.gpsimd.memset(eye8[:, :], 0.0).then_inc(s_const, 1)
            pool.wait_ge(s_const, 3)
            nc.gpsimd.affine_select(out=eye8[:, :], in_=eye8[:, :], compare_op=ALU.not_equal, fill=1.0, base=0,
                                    pattern=[[-1, B]], channel_multiplier=1).then_inc(s_const, 1)
            nc.gpsimd.affine_select(out=ident[:, :], in_=ident[:, :], compare_op=ALU.not_equal, fill=1.0, base=0,
                                    pattern=[[-1, C]], channel_multiplier=1).then_inc(s_const, 1)
            nc.gpsimd.memset(ones[:, :], 1.0).then_inc(s_const, 1)
            nc.gpsimd.memset(ones_row[:, :], 1.0).then_inc(s_const, 1)
            nc.gpsimd.memset(v_all[:, :, :, :, D:VW], 1.0).then_inc(s_const, 1)

            def fill(c):
                for stack, word in ((k_stack, ONES_BF16), (q_stack[0], 0), (q_stack[1], 0)):
                    nc.gpsimd.memset(stack[:, c, :, :].rearrange("p g t -> p (g t)").bitcast(U32), word)\
                      .then_inc(s_fill, 1)

            for c in range(NC):
                fill(c)

            for k in range(HALVES):
                pool.wait_ge(s_ad, unit_item(4 * k + 3) + 2)
                if k >= 2:
                    pool.wait_ge(s_a, turn_item(k - 2) + 1)
                neg = neg_max[:, k % 2, :, :, :]
                nc.gpsimd.tensor_copy(max_parts[:, k % 2, :, :, 0, :], neg).then_inc(s_mp, 1)
                pool.wait_ge(s_mp, 2 * k + 1)
                nc.gpsimd.tensor_tensor(max_parts[:, k % 2, :, :, 1, :], neg, max_parts[:, k % 2, :, :, 0, :],
                                        ALU.subtract).then_inc(s_mp, 1)
                pool.wait_ge(s_ad, turn_item(k) + 1)
                c, at = divmod(k // 2, BC)
                for par in range(2):
                    pool.dma_start(q_stack[par][ROW_MAX:ROW_MAX + 2, c, 4 * (k % 2):4 * (k % 2) + 4, at * N:(at + 1) * N],
                                   max_rows[8 * par:8 * par + 8, k % 2, :]).then_inc(s_mr[k % 2], 16)

        @block.tensor
        def _(pe):
            pe.wait_ge(s_wa, 48)
            pe.wait_ge(s_cond, 2)
            nc.tensor.matmul(bank[:, 0, 0:B], scale_w[:, :], cond[:, :], start=True, stop=True)
            nc.tensor.matmul(bank[:, 1, 0:B], shift_w[:, :], cond[:, :], start=True, stop=True).then_inc(s_small, 1)
            pe.wait_ge(s_const, 6)
            pe.wait_ge(s_tab, 5)
            nc.tensor.matmul(bank[:, 2, 0:B], ones[:, :], any_diag[:, :], start=True, stop=True).then_inc(s_small, 1)

            def mean_square(c):
                pe.wait_ge(s_sq, c + 1)
                if c >= 2:
                    pe.wait_ge(s_rs, c - 1)
                nc.tensor.matmul(bank[:, 3 + c % 2, :], mean_w[:, :], sq[:, c % 2, :],
                                 start=True, stop=True).then_inc(s_ss, 1)

            def qkv(c):
                pe.wait_ge(s_h, BC * (c + 1))
                for i in range(2):
                    if c >= 1:
                        pe.wait_ge(s_rest[i], (BC, 1)[i] * c)
                    nc.tensor.matmul(bank[:, 5 + i, :], qkv_w[:, i * C:(i + 1) * C], h[:, c % 2, :],
                                     start=True, stop=True).then_inc(s_qk, 1)
                if c >= 1:
                    pe.wait_ge(s_v_out, c)
                for t in range(CH // C):
                    mm = nc.tensor.matmul(bank[:, 7, t * C:(t + 1) * C], h[:, c % 2, t * C:(t + 1) * C],
                                          qkv_w[:, 2 * C:3 * C], start=True, stop=True)
                mm.then_inc(s_v, 1)

            def query_scores(u, heads=(0, 1)):
                b, g = divmod(u, G)
                c, at = b // BC, (b % BC) * N
                if u % (BC * G) == 0 and heads[0] == 0:
                    pe.wait_ge(s_stack[c], 16 * 7)
                for par in heads:
                    n = unit_item(u) + par
                    if n >= RING:
                        pe.wait_ge(s_ad, n - RING + 1)
                    for t in range(KT):
                        mm = nc.tensor.matmul(bank[:, n % RING, t * N:(t + 1) * N],
                                              q_stack[par][:, c, g, at + t * 128:at + (t + 1) * 128],
                                              k_stack[:, c, g, at:at + N],
                                              start=True, stop=True)
                    mm.then_inc(s_a, 1)

            def turn_maxima(k):
                n = turn_item(k)
                pe.wait_ge(s_ad, n - RING + 1)
                pe.wait_ge(s_mp, 2 * (k + 1))
                for t in range(KT):
                    mm = nc.tensor.transpose(bank[0:2 * G, n % RING, t * 64:(t + 1) * 64].bitcast(BF16),
                                             max_parts[:, k % 2, t, :, :, :].rearrange("p r j g -> p (r j g)"),
                                             ident[:, :])
                mm.then_inc(s_a, 1)

            def key_scores(u, par):
                b, g = divmod(u, G)
                c, at = b // BC, (b % BC) * N
                v = 2 * u + par
                if v % 8 == 0:
                    k = u // 4
                    pe.wait_ge(s_mr[k % 2], 32 * (k // 2 + 1))
                if v >= RING:
                    pe.wait_ge(s_e, v - RING + 1)
                for t in range(KT):
                    mm = nc.tensor.matmul(bank[:, RING + v % RING, t * N:(t + 1) * N],
                                          k_stack[:, c, g, at + t * 128:at + (t + 1) * 128],
                                          q_stack[par][:, c, g, at:at + N], start=True, stop=True)
                mm.then_inc(s_b, 1)

            def p_times_v(q, t):
                b, g = divmod(2 * q, G)
                k = q // 2
                if t == 0:
                    pe.wait_ge(s_e, 4 * q + 4)
                    if q == 0:
                        pe.wait_ge(s_const, 8)
                        pe.wait_ge(s_v_out, NC)
                        pe.wait_ge(s_zero, 1)
                    if q % 2 == 0 and k >= 2:
                        pe.wait_ge(s_od, k - 1)
                for j in range(4):
                    mm = nc.tensor.matmul(bank[32 * j:32 * j + VW, 6 + k % 2, (q % 2) * N:(q % 2 + 1) * N],
                                          v_all[:, b, t, 2 * g + j, :],
                                          p_exp[:, (2 * q + j // 2) % 4, j % 2, t, :],
                                          start=(t == 0), stop=(t == KT - 1), tile_position=(0, 32 * j))
                if t == KT - 1:
                    mm.then_inc(s_pv, 1)

            def project(c):
                pe.wait_ge(s_on, c + 1)
                if c == 0:
                    pe.wait_ge(s_wb, 48)
                    pe.wait_ge(s_ad, turn_item(HALVES - 1) + 1)
                if c == 2:
                    pe.wait_ge(s_y, 1)
                if c == 3:
                    pe.wait_ge(s_rs2, 2)
                nc.tensor.matmul(bank[:, c % 2 if c < 3 else 0, :], proj_w[:, :], o_num[:, c, :],
                                 start=True, stop=True).then_inc(s_proj, 1)

            def mean_square_2(c):
                pe.wait_ge(s_sq2, c + 1)
                if c < 2:
                    pe.wait_ge(s_y, c + 2)
                else:
                    pe.wait_ge(s_rs2, 2 * c - 3)
                nc.tensor.matmul(bank[:, (c + 1) % 2 if c < 3 else 1, :], mean_w[:, :], sq2[:, c % 2, :],
                                 start=True, stop=True).then_inc(s_ss2, 1)

            def mlp_in(n):
                c, m = divmod(n, MT)
                if m == 0:
                    pe.wait_ge(s_h2, BC * (c + 1))
                if n < 2:
                    pe.wait_ge(s_e, 2 * UNITS)
                else:
                    pe.wait_ge(s_gated, n - 1)
                for i in range(2):
                    nc.tensor.matmul(bank[:, 2 + 2 * (n % 2) + i, :], w1[:, i * MLP + m * C:i * MLP + (m + 1) * C],
                                     h2[:, c, :], start=True, stop=True).then_inc(s_w1, 1)

            def mlp_out(n):
                c, m = divmod(n, MT)
                pe.wait_ge(s_gated, n + 1)
                if n == 0:
                    pe.wait_ge(s_od, HALVES)
                if m == 0 and c >= 2:
                    pe.wait_ge(s_out, c - 1)
                mm = nc.tensor.matmul(bank[:, 6 + c % 2, :], w2[:, m, :], gated[:, n % 3, :],
                                      start=(m == 0), stop=(m == MT - 1))
                if m == MT - 1:
                    mm.then_inc(s_w2, 1)

            mean_square(0)
            mean_square(1)
            mean_square(2)
            qkv(0)
            mean_square(3)
            qkv(1)
            qkv(2)
            for u in range(4):
                query_scores(u)
            qkv(3)
            for u in range(4, G):
                query_scores(u)
                if u == 4:
                    turn_maxima(0)
            for u in range(UNITS):
                if u + G < UNITS:
                    query_scores(u + G, heads=(0,))
                key_scores(u, 0)
                if u + G < UNITS:
                    query_scores(u + G, heads=(1,))
                key_scores(u, 1)
                if u % 4 == 0 and u < UNITS - 4:
                    turn_maxima(u // 4 + 1)
                if u >= LAG:
                    p_times_v((u - LAG) // 2, (u - LAG) % 2)
                if UNITS - G <= u < UNITS - G + 3:
                    project(u - (UNITS - G))
                if UNITS - G + 3 <= u < UNITS - G + 6:
                    mean_square_2(u - (UNITS - G) - 3)
            for u in range(UNITS - LAG, UNITS):
                p_times_v(u // 2, u % 2)

            for n in range(NC * MT):
                mlp_in(n)
                if n >= 1:
                    mlp_out(n - 1)
                if n == LATE:
                    project(NC - 1)
                if n == LATE + 2:
                    mean_square_2(NC - 1)
            mlp_out(NC * MT - 1)

        @block.scalar
        def _(act):
            nc.scalar.preload_act_table_set("natural_log_exp_and_others")
            act.wait_ge(s_in, 48)
            nc.scalar.activation(sig[:, :], c_sb[:, :], ACT.Exp, scale=-1.0).then_inc(s_sig, 1)

            def square(c):
                act.wait_ge(s_x[c], 16)
                if c >= 2:
                    act.wait_ge(s_ss, c - 1)
                nc.scalar.activation(sq[:, c % 2, :], x_sb[:, c * CH:(c + 1) * CH], ACT.Square).then_inc(s_sq, 1)

            def power(t, exponent, s, n):
                nc.scalar.activation(t, t, ACT.Ln).then_inc(s, 1)
                act.wait_ge(s, n)
                nc.scalar.activation(t, t, ACT.Exp, scale=exponent).then_inc(s, 1)

            def inverse_norm(c):
                act.wait_ge(s_rs, c + 1)
                power(rs[:, c, :], -0.5, s_inv, 2 * c + 1)

            def shifted(c):
                for b in range(BC * c, BC * c + BC):
                    at = (b % BC) * N
                    act.wait_ge(s_xn, b + 1)
                    if c >= 2:
                        act.wait_ge(s_v, c - 1)
                    nc.scalar.activation(h[:, c % 2, at:at + N], xn[:, c % 2, at:at + N], ACT.Identity,
                                         bias=shift[:, b:b + 1]).then_inc(s_h, 1)

            def first_parts(c):
                if c >= 2:
                    act.wait_ge(s_pw[c % 2], 96 * (c // 2))
                act.wait_ge(s_qk, 2 * c + 1)
                for i in range(BC):
                    nc.scalar.activation(parts[:, c % 2, 0, 0, i * N:(i + 1) * N], bank[:, 5, i * N:(i + 1) * N],
                                         ACT.Copy, scale=any_all[:, BC * c + i:BC * c + i + 1]).then_inc(s_part0[0], 1)
                act.wait_ge(s_qk, 2 * c + 2)
                nc.scalar.activation(parts[:, c % 2, 1, 0, :], bank[:, 6, :], ACT.Copy).then_inc(s_part0[1], 1)

            def values(c):
                act.wait_ge(s_v, c + 1)
                nc.scalar.activation(v_all[:, BC * c:BC * (c + 1), :, :, 0:D],
                                     bank[:, 7, :].rearrange("p (b t h d) -> p b t h d", b=BC, t=KT, h=H),
                                     ACT.Copy).then_inc(s_v_out, 1)

            square(0)
            square(1)
            inverse_norm(0)
            square(2)
            act.wait_ge(s_tab, 9)
            shifted(0)
            inverse_norm(1)
            square(3)
            shifted(1)
            first_parts(0)
            values(0)
            inverse_norm(2)
            shifted(2)
            first_parts(1)
            values(1)
            inverse_norm(3)
            shifted(3)
            for c in range(2, NC):
                first_parts(c)
                values(c)

            def drain_output(k):
                act.wait_ge(s_pv, 2 * k + 2)
                if k >= 2:
                    act.wait_ge(s_ow[k % 2], 16 * (k // 2))
                nc.scalar.activation(o_sb[:, k % 2, :], bank[:, 6 + k % 2, :], ACT.Copy).then_inc(s_od, 1)

            def inverse_sum(c):
                act.wait_ge(s_or[c], 32 * BC)
                power(o_den[:, c, :], -1.0, s_rec, 2 * c + 1)

            def square_2(c):
                act.wait_ge(s_y, c + 1)
                if c >= 2:
                    act.wait_ge(s_ss2, c - 1)
                nc.scalar.activation(sq2[:, c % 2, :], y[:, c, :], ACT.Square).then_inc(s_sq2, 1)

            def inverse_norm_2(c):
                act.wait_ge(s_rs2, c + 1)
                power(rs2[:, c, :], -0.5, s_inv2, 2 * c + 1)

            def shifted_2(c):
                for b in range(BC * c, BC * c + BC):
                    at = (b % BC) * N
                    act.wait_ge(s_xn2, b + 1)
                    nc.scalar.activation(h2[:, c, at:at + N], xn2[:, c, at:at + N], ACT.Identity,
                                         bias=shift[:, b:b + 1]).then_inc(s_h2, 1)

            for u in range(UNITS):
                if u >= 4:
                    act.wait_ge(s_pv, u // 2 - 1)
                for par in range(2):
                    v = 2 * u + par
                    act.wait_ge(s_b, v + 1)
                    nc.scalar.activation(p_exp[:, u % 4, par, :, :],
                                         bank[:, RING + v % RING, :].rearrange("p (t q) -> p t q", t=KT),
                                         ACT.Exp, scale=D ** -0.5).then_inc(s_e, 1)
                if u % 4 == 2 and u >= 6:
                    drain_output(u // 4 - 1)
                if u % 16 == 8 and u >= 16:
                    inverse_sum(u // 16 - 1)
                if UNITS - 5 <= u < UNITS - 2:
                    square_2(u - (UNITS - 5))
                if u == UNITS - 1:
                    inverse_norm_2(0)
            drain_output(HALVES - 1)
            shifted_2(0)
            for c in range(1, NC - 1):
                inverse_norm_2(c)
                shifted_2(c)

            for n in range(NC * MT):
                m = n % MT
                act.wait_ge(s_w1, 2 * n + 1)
                if n >= 2:
                    act.wait_ge(s_silu, n - 1)
                nc.scalar.activation(x1_half[:, n % 2, :], bank[:, 2 + 2 * (n % 2), :], ACT.Identity,
                                     bias=half_b1[:, m:m + 1], scale=0.5).then_inc(s_th, 1)
                nc.scalar.activation(th[:, n % 2, :], bank[:, 2 + 2 * (n % 2), :], ACT.Tanh,
                                     bias=half_b1[:, m:m + 1], scale=0.5).then_inc(s_th, 1)
                if n == LATE - 1:
                    inverse_sum(NC - 1)
                if n == LATE + 1:
                    square_2(NC - 1)
                if n == LATE + 3:
                    inverse_norm_2(NC - 1)
                if n == LATE + 4:
                    shifted_2(NC - 1)

        @block.vector
        def _(dve):
            dve.wait_ge(s_in, 48)
            nc.vector.tensor_scalar(half_b1[:, :], vec[:, V_B1:V_B1 + MT], 0.5, None, ALU.mult).then_inc(s_tab, 1)
            nc.vector.tensor_scalar(valid[:, :], mask_sb[:, :], 0.0, None, ALU.not_equal).then_inc(s_tab, 1)
            dve.wait_ge(s_sig, 1)
            nc.vector.tensor_scalar(sig[:, :], sig[:, :], 1.0, None, ALU.add).then_inc(s_tab, 1)
            dve.wait_ge(s_tab, 3)
            nc.vector.tensor_reduce(out=any_valid[:, :], in_=valid[:, :], axis=AX.X, op=ALU.max).then_inc(s_tab, 1)
            dve.wait_ge(s_tab, 4)
            nc.vector.reciprocal(sig[:, :], sig[:, :]).then_inc(s_cond, 1)
            dve.wait_ge(s_cond, 1)
            nc.vector.tensor_tensor(cond[:, :], c_sb[:, :], sig[:, :], ALU.mult).then_inc(s_cond, 1)
            dve.wait_ge(s_const, 5)
            nc.vector.tensor_scalar(any_diag[:, :], eye8[:, :], any_valid[:, :], None, ALU.mult).then_inc(s_tab, 1)
            nc.vector.tensor_scalar(valid[:, :], valid[:, :], 1.0, -MASKED, ALU.subtract, ALU.mult).then_inc(s_cond, 1)
            dve.wait_ge(s_cond, 3)
            nc.vector.tensor_scalar(mask_add[:, :], valid[:, :], any_valid[:, :], None, ALU.mult).then_inc(s_tab, 1)
            dve.wait_ge(s_small, 2)
            nc.vector.tensor_copy(any_all[:, :], bank[:, 2, 0:B]).then_inc(s_tab, 1)
            nc.vector.tensor_scalar(shift[:, :], bank[:, 1, 0:B], vec[:, V_SHIFT_B:V_SHIFT_B + 1], None,
                                    ALU.add).then_inc(s_tab, 1)
            nc.vector.tensor_scalar(gain[:, :], bank[:, 0, 0:B], vec[:, V_SCALE_B:V_SCALE_B + 1], 1.0,
                                    ALU.add, ALU.add).then_inc(s_tab, 1)
            dve.wait_ge(s_tab, 9)
            nc.vector.tensor_scalar(gain[:, :], gain[:, :], 0.1, 10.0, ALU.max, ALU.min).then_inc(s_tab, 1)
            dve.wait_ge(s_tab, 10)
            nc.vector.tensor_scalar(gain[:, :], gain[:, :], vec[:, V_NORM:V_NORM + 1], None, ALU.mult).then_inc(s_tab, 1)
            dve.wait_ge(s_tab, 11)

            def guard(c):
                dve.wait_ge(s_ss, c + 1)
                nc.vector.tensor_scalar(rs[:, c, :], bank[:, 3 + c % 2, :], EPS * EPS, None,
                                        ALU.max).then_inc(s_rs, 1)

            def norm(c):
                dve.wait_ge(s_inv, 2 * c + 2)
                for i in range(BC):
                    b = BC * c + i
                    if c >= 2:
                        dve.wait_ge(s_h, b - 3)
                    nc.vector.scalar_tensor_tensor(out=xn[:, c % 2, i * N:(i + 1) * N],
                                                   in0=x_sb[:, b * N:(b + 1) * N], scalar=gain[:, b:b + 1],
                                                   in1=rs[:, c, i * N:(i + 1) * N],
                                                   op0=ALU.mult, op1=ALU.mult).then_inc(s_xn, 1)

            def split(c):
                q_part, k_part, rest_q, rest_k = parts[:, c % 2, 0, :, :], parts[:, c % 2, 1, :, :], *(
                    rest[:, c % 2, i, :] for i in range(2))
                dve.wait_ge(s_part0[0], BC * (c + 1))
                for i in range(BC):
                    at = slice(i * N, (i + 1) * N)
                    nc.vector.scalar_tensor_tensor(out=rest_q[:, at], in0=bank[:, 5, at],
                                                   scalar=any_all[:, BC * c + i:BC * c + i + 1], in1=q_part[:, 0, at],
                                                   op0=ALU.mult, op1=ALU.subtract).then_inc(s_rest[0], 1)
                dve.wait_ge(s_part0[1], c + 1)
                nc.vector.tensor_tensor(rest_k, bank[:, 6, :], k_part[:, 0, :], ALU.subtract).then_inc(s_rest[1], 1)
                dve.wait_ge(s_rest[0], BC * (c + 1))
                nc.vector.tensor_copy(q_part[:, 1, :], rest_q).then_inc(s_split[0], 1)
                dve.wait_ge(s_rest[1], c + 1)
                nc.vector.tensor_copy(k_part[:, 1, :], rest_k).then_inc(s_split[1], 1)
                dve.wait_ge(s_split[0], 2 * c + 1)
                nc.vector.tensor_tensor(q_part[:, 2, :], rest_q, q_part[:, 1, :], ALU.subtract).then_inc(s_split[0], 1)
                dve.wait_ge(s_split[1], 2 * c + 1)
                nc.vector.tensor_tensor(k_part[:, 2, :], rest_k, k_part[:, 1, :], ALU.subtract).then_inc(s_split[1], 1)

            def maxima(u):
                k, g = divmod(u, 4)
                if g == 0 and k >= 2:
                    dve.wait_ge(s_mp, 2 * (k - 1))
                for par in range(2):
                    n = unit_item(u) + par
                    dve.wait_ge(s_a, n + 1)
                    nc.vector.tensor_reduce(out=neg_max[:, k % 2, :, par, g],
                                            in_=bank[:, n % RING, :].rearrange("p (t k) -> p t k", t=KT),
                                            axis=AX.X, op=ALU.max, negate=True).then_inc(s_ad, 1)

            def turned(k):
                n = turn_item(k)
                dve.wait_ge(s_a, n + 1)
                if k >= 2:
                    dve.wait_ge(s_mr[k % 2], 32 * (k // 2))
                nc.vector.tensor_copy(max_rows[:, k % 2, :],
                                      bank[0:2 * G, n % RING, 0:2 * 64].bitcast(BF16)).then_inc(s_ad, 1)

            def over_sum(c):
                dve.wait_ge(s_rec, 2 * c + 2)
                nc.vector.tensor_tensor(o_num[:, c, :], o_num[:, c, :], o_den[:, c, :], ALU.mult).then_inc(s_on, 1)

            def residual(c):
                dve.wait_ge(s_proj, c + 1)
                nc.vector.scalar_tensor_tensor(out=y[:, c, :], in0=bank[:, c % 2 if c < 3 else 0, :],
                                               scalar=vec[:, V_PROJ_B:V_PROJ_B + 1],
                                               in1=x_sb[:, c * CH:(c + 1) * CH], op0=ALU.add, op1=ALU.add).then_inc(s_y, 1)

            def guard_2(c):
                dve.wait_ge(s_ss2, c + 1)
                nc.vector.tensor_scalar(rs2[:, c, :], bank[:, (c + 1) % 2 if c < 3 else 1, :], EPS * EPS, None,
                                        ALU.max).then_inc(s_rs2, 1)

            def norm_2(c):
                dve.wait_ge(s_inv2, 2 * c + 2)
                for i in range(BC):
                    b = BC * c + i
                    nc.vector.scalar_tensor_tensor(out=xn2[:, c, i * N:(i + 1) * N],
                                                   in0=y[:, c, i * N:(i + 1) * N], scalar=gain[:, b:b + 1],
                                                   in1=rs2[:, c, i * N:(i + 1) * N],
                                                   op0=ALU.mult, op1=ALU.mult).then_inc(s_xn2, 1)

            def add_out(c):
                dve.wait_ge(s_w2, c + 1)
                nc.vector.scalar_tensor_tensor(out=out_sb[:, c, :], in0=bank[:, 6 + c % 2, :],
                                               scalar=vec[:, V_B2:V_B2 + 1], in1=y[:, c, :],
                                               op0=ALU.add, op1=ALU.add).then_inc(s_out, 1)

            guard(0)
            guard(1)
            norm(0)
            guard(2)
            norm(1)
            split(0)
            guard(3)
            norm(2)
            split(1)
            norm(3)
            split(2)
            for u in range(4):
                maxima(u)
            split(3)
            dve.wait_ge(s_v_out, NC)
            nc.vector.memset(bank[:, 6:8, :], 0.0).then_inc(s_zero, 1)
            for u in range(4, UNITS):
                maxima(u)
                if u % 4 == 0:
                    turned(u // 4 - 1)
                if u % 16 == 1 and u >= 33:
                    over_sum(u // 16 - 2)
            turned(HALVES - 1)
            over_sum(2)
            for c in range(3):
                residual(c)
            for c in range(3):
                guard_2(c)
            for c in range(3):
                norm_2(c)

            for n in range(NC * MT):
                c, m = divmod(n, MT)
                dve.wait_ge(s_th, 2 * n + 2)
                nc.vector.scalar_tensor_tensor(out=silu[:, n % 2, :], in0=th[:, n % 2, :], scalar=1.0,
                                               in1=x1_half[:, n % 2, :], op0=ALU.add, op1=ALU.mult).then_inc(s_silu, 1)
                dve.wait_ge(s_silu, n + 1)
                dve.wait_ge(s_w1, 2 * n + 2)
                b1 = vec[:, V_B1 + MT + m:V_B1 + MT + m + 1]
                nc.vector.scalar_tensor_tensor(out=gated[:, n % 3, :], in0=bank[:, 3 + 2 * (n % 2), :], scalar=b1,
                                               in1=silu[:, n % 2, :], op0=ALU.add, op1=ALU.mult).then_inc(s_gated, 1)
                if n == LATE - 1:
                    over_sum(NC - 1)
                if n == LATE:
                    residual(NC - 1)
                if n == LATE + 2:
                    guard_2(NC - 1)
                if n == LATE + 3:
                    norm_2(NC - 1)
                if m == 0 and c >= 1:
                    add_out(c - 1)
            add_out(NC - 1)


def kernel(x, cond_1024, mask_BxS_ik0, L0_cond_norm_w, L0_cond_scale_w, L0_cond_scale_b, L0_cond_shift_w,
           L0_cond_shift_b, L0_cond_qkv_w, L0_cond_proj_w, L0_cond_proj_b, L0_cond_mlp_w1, L0_cond_mlp_b1,
           L0_cond_mlp_w2, L0_cond_mlp_b2):
    import numpy as np
    import concourse.bacc as bacc
    from concourse.bass_utils import run_bass_kernel_spmd

    def turned(a):
        return np.ascontiguousarray(np.asarray(a).T)

    vectors = [np.asarray(v).reshape(-1, C) for v in
               (L0_cond_norm_w, L0_cond_scale_b, L0_cond_shift_b, L0_cond_proj_b, L0_cond_mlp_b2, L0_cond_mlp_b1)]
    w2 = np.asarray(L0_cond_mlp_w2).T.reshape(MT, C, C).transpose(1, 0, 2)
    arrays = {
        "x_t": turned(np.asarray(x).reshape(TOK, C)),
        "c_t": turned(cond_1024),
        "mask": np.ascontiguousarray(mask_BxS_ik0),
        "vecs": turned(np.concatenate(vectors, axis=0)),
        "scale_wt": turned(L0_cond_scale_w),
        "shift_wt": turned(L0_cond_shift_w),
        "qkv_wt": turned(L0_cond_qkv_w),
        "proj_wt": turned(L0_cond_proj_w),
        "w1_t": turned(L0_cond_mlp_w1),
        "w2_t": np.ascontiguousarray(w2),
    }
    nc = bacc.Bacc("TRN2", target_bir_lowering=False, num_devices=1)
    args = [nc.dram_tensor(name, a.shape, mybir.dt.from_np(a.dtype), kind="ExternalInput").ap()
            for name, a in arrays.items()]
    out_t = nc.dram_tensor("out_t", (C, TOK), F32, kind="ExternalOutput").ap()
    build(nc, *args, out_t)
    result = run_bass_kernel_spmd(nc, [arrays], core_ids=[0]).results[0]["out_t"]
    return np.ascontiguousarray(result.T).reshape(B, N, C)
```

```python
from contextlib import ExitStack

import concourse.bass as bass
from concourse import mybir

F32 = mybir.dt.float32
F32R = mybir.dt.float32r
BF16 = mybir.dt.bfloat16
I32 = mybir.dt.int32
U32 = mybir.dt.uint32
ALU = mybir.AluOpType
ACT = mybir.ActivationFunctionType
AX = mybir.AxisListType

C = 128
B, N = 8, 256
TOK = B * N
H, D = 16, 8
MLP = 4 * C
G = H // 2
CH = 512
NC = TOK // CH
BC = CH // N
KT = N // 128
WARM = (8, 2)
VW = D + 1
EPS = 1e-6
MASKED = -float(2 ** 100)
ONES_BF16 = 0x3F803F80

Q_PARTS = [0, 0, 0, 1, 1, 2]
K_PARTS = [0, 1, 2, 0, 1, 0]
SLOTS = len(Q_PARTS)
HEAD_ROWS = D * SLOTS
ROW_MASK = 2 * HEAD_ROWS
ROW_MAX = ROW_MASK + 1
HALVES = 2 * B
UNITS = B * G

MT = MLP // C
LEAD = 8
P_LN_SUM, P_INVERSE_SUM, P_OVER_SUM, P_PROJECT, P_SQUARE, P_MEAN, P_LN_NORM, P_INVERSE_NORM, P_NORM, P_SHIFT, \
    P_SECOND_PART = (7, 8, 9, 10, 12, 13, 15, 16, 17, 19, 22)
RING = 3
LAG = 2
AT_INVERSE_SUM, AT_OVER_SUM, AT_PROJECT, AT_RESIDUAL, AT_SQUARE, AT_MEAN, AT_GUARD, AT_INVERSE_NORM, AT_NORM, \
    AT_SHIFT, AT_SECOND_PART = (3, 3, 5, 5, 6, 7, 7, 8, 8, 9, 9)
OUT_LAG = 3
SPLIT_PAIRS = NC * MLP // C - 2
GB = OUT_LAG + 1

V_NORM, V_SCALE_B, V_SHIFT_B, V_PROJ_B, V_B2, V_B1 = 0, 1, 2, 3, 4, 5
NVEC = V_B1 + 2 * MLP // C


def turn_position(k):
    return 4 * k + 4


def project_position(c):
    return BC * G * (c + 1) + LEAD + P_PROJECT


def square_position(c):
    return BC * G * (c + 1) + LEAD + P_MEAN


def ring_items():
    items = []
    for p in range(UNITS + LEAD):
        if p < UNITS:
            items += [("scores", p, 0), ("scores", p, 1)]
        items += [("turn", k) for k in range(HALVES) if turn_position(k) == p]
        items += [("project", c) for c in range(NC - 1) if project_position(c) == p]
        items += [("square", c) for c in range(NC - 1) if square_position(c) == p]
    return items


ITEMS = ring_items()

SLOTS_MLP = list(range(AT_PROJECT + 1)) + ["project"] + list(range(AT_PROJECT + 1, AT_MEAN + 1)) + ["square"] + \
    list(range(AT_MEAN + 1, NC * MT))


def item(*what):
    return ITEMS.index(what)


def build(nc, x_t, small, mask, front_w, back_w, out_t):
    q_rows = nc.dram_tensor("q_rows", [C, SLOTS, TOK], BF16).ap()
    k_rows = nc.dram_tensor("k_rows", [C, SLOTS, TOK], BF16).ap()
    o_rows = nc.dram_tensor("o_rows", [B, H, 32, N], F32).ap()

    ctx = ExitStack()
    with ctx:
        def sb(name, shape, dt=F32):
            return ctx.enter_context(nc.sbuf_tensor(name, shape, dt))

        def sem(name):
            return ctx.enter_context(nc.semaphore(name))

        x_sb = sb("x_sb", [C, TOK])
        small_sb = sb("small_sb", [C, NVEC + B])
        vec, c_sb = small_sb[:, 0:NVEC], small_sb[:, NVEC:NVEC + B]
        mask_sb = sb("mask_sb", [B, N], I32)
        front = sb("front", [C, 5 * C])
        scale_w, shift_w, qkv_w = front[:, 0:C], front[:, C:2 * C], front[:, 2 * C:5 * C]
        back = sb("back", [C, C + 3 * MLP])
        proj_w, w_mlp = back[:, 0:C], back[:, C:C + 3 * MLP]
        mean_w = sb("mean_w", [C, C])
        ones = sb("ones", [B, C])
        ident = sb("ident", [C, C], BF16)
        eye8 = sb("eye8", [B, B])
        ones_row = sb("ones_row", [1, CH], BF16)
        zero_row = sb("zero_row", [1, C], BF16)
        words = sb("words", [C, 2])
        sig = sb("sig", [C, B])
        cond = sb("cond", [C, B])
        gain = sb("gain", [C, B])
        shift = sb("shift", [C, B])
        valid = sb("valid", [B, N])
        any_valid = sb("any_valid", [B, 1])
        any_diag = sb("any_diag", [B, B])
        mask_add = sb("mask_add", [B, N], BF16)
        any_all = sb("any_all", [C, B])
        sq = sb("sq", [C, 2, CH])
        rs = sb("rs", [C, NC, CH])
        xn = sb("xn", [C, 2, CH])
        h = sb("h", [C, 2, CH])
        o_den = sb("o_den", [C, NC, CH])
        rest = sb("rest", [C, 2, 2, CH])
        parts = sb("parts", [C, 2, 2, 3, CH], BF16)
        v_all = sb("v_all", [C, B, KT, H, VW])
        neg_max = sb("neg_max", [C, 2, KT, G // 2, 2])
        max_parts = sb("max_parts", [C, 2, KT, 2, G // 2, 2], BF16)
        max_rows = sb("max_rows", [2 * G, 2, N], BF16)
        p_exp = sb("p_exp", [C, 4, 2, KT, N])
        o_sb = sb("o_sb", [C, 2, CH])
        o_num = sb("o_num", [C, NC, CH])
        y = rest.rearrange("p c i t -> p (c i) t")
        sq2 = sq
        rs2 = parts.rearrange("p c i j t -> p (c i j t)").bitcast(F32)[:, 0:NC * CH].rearrange("p (c t) -> p c t", c=NC)
        xn2 = o_den
        out_sb = o_num

        sig_x1, gated = h, rs
        silu = xn
        with ExitStack() as stacks:
            k_stack = stacks.enter_context(nc.sbuf_tensor("k_stack", [C, NC, G, CH], BF16))
            q_stack = stacks.enter_context(nc.sbuf_tensor("q_stack", [C, NC, G, 2, CH], BF16))
        h2_hi = sb("h2_hi", [C, G // 2, CH], F32R)
        h2_lo = sb("h2_lo", [C, G // 2, CH], F32R)
        sb("k_stack_2_and_3", [C, G, CH])
        w_parts = sb("w_parts", [C, G, CH], F32R)
        gated_hi = sb("gated_hi", [C, G // 2, CH], F32R)
        gated_lo = sb("gated_lo", [C, G // 2, CH], F32R)
        sb("q_stack_2_and_3", [C, 2 * G, CH])

        bank = ctx.enter_context(nc.psum_tensor("bank", [C, 8, CH], F32))

        s_in = sem("s_in")
        s_x = [sem(f"s_x{c}") for c in range(NC)]
        s_wa = sem("s_wa")
        s_wb = sem("s_wb")
        s_const = sem("s_const")
        s_fill0 = sem("s_fill0")
        s_fill = sem("s_fill")
        s_words = sem("s_words")
        s_sig = sem("s_sig")
        s_cond = sem("s_cond")
        s_small = sem("s_small")
        s_gain = sem("s_gain")
        s_shift = sem("s_shift")
        s_any = sem("s_any")
        s_mask = sem("s_mask")
        s_sq = sem("s_sq")
        s_ss = sem("s_ss")
        s_rs = sem("s_rs")
        s_inv = sem("s_inv")
        s_inv2 = sem("s_inv2")
        s_rec = sem("s_rec")
        s_xn = sem("s_xn")
        s_h = sem("s_h")
        s_qk = sem("s_qk")
        s_v = sem("s_v")
        s_part0 = [sem("s_part0_q"), sem("s_part0_k")]
        s_rest = [sem("s_rest_q"), sem("s_rest_k")]
        s_v_out = sem("s_v_out")
        s_split = [sem("s_split_q"), sem("s_split_k")]
        s_last = [sem("s_last_q"), sem("s_last_k")]
        s_qw = [sem(f"s_qw{i}") for i in range(2)]
        s_kw = [sem(f"s_kw{i}") for i in range(2)]
        s_stack = [sem(f"s_stack{c}") for c in range(NC)]
        s_a = sem("s_a")
        s_ad = sem("s_ad")
        s_mp = sem("s_mp")
        s_mr = [sem(f"s_mr{i}") for i in range(2)]
        s_b = sem("s_b")
        s_e = sem("s_e")
        s_pv = sem("s_pv")
        s_od = sem("s_od")
        s_ow = [sem(f"s_ow{i}") for i in range(2)]
        s_or = [sem(f"s_or{c}") for c in range(NC)]
        s_on = sem("s_on")
        s_proj = sem("s_proj")
        s_sq2 = sem("s_sq2")
        s_ss2 = sem("s_ss2")
        s_y3 = sem("s_y3")
        s_rs3 = sem("s_rs3")
        s_xn2 = sem("s_xn2")
        s_h2 = sem("s_h2")
        s_h2_lo = sem("s_h2_lo")
        s_w_parts = sem("s_w_parts")
        s_w1 = sem("s_w1")
        s_sig_x1 = sem("s_sig_x1")
        s_silu = sem("s_silu")
        s_gated = sem("s_gated")
        s_gated_hi = sem("s_gated_hi")
        s_gated_lo = sem("s_gated_lo")
        s_w2 = sem("s_w2")
        s_out = sem("s_out")
        s_store = sem("s_store")

        block = ctx.enter_context(nc.Block())

        @block.sync
        def _(sp):
            sp.dma_start(x_sb[:, 0:CH], x_t[:, 0:CH]).then_inc(s_x[0], 16)
            sp.dma_start(small_sb[:, :], small).then_inc(s_in, 16)
            sp.dma_start(mask_sb[:, :], mask).then_inc(s_in, 16)
            sp.dma_start(front[:, :], front_w).then_inc(s_wa, 16)
            for c in range(1, NC):
                sp.dma_start(x_sb[:, c * CH:(c + 1) * CH], x_t[:, c * CH:(c + 1) * CH]).then_inc(s_x[c], 16)
            sp.dma_start(back[:, :], back_w).then_inc(s_wb, 16)

            for c in range(NC):
                tok = slice(c * CH, (c + 1) * CH)
                if c == 0:
                    sp.wait_ge(s_const, 7)
                    sp.wait_ge(s_mask, 5)
                sp.wait_ge(*((s_fill0, 3), (s_fill, 2 * c))[c >= 1])
                for i in range(BC):
                    b = BC * c + i
                    sp.dma_start(k_stack[ROW_MASK:ROW_MASK + 1, c, :, i * N:(i + 1) * N],
                                 mask_add[b:b + 1, :].unsqueeze(1).to_broadcast([1, G, N])).then_inc(s_stack[c], 16)
                sp.dma_start(q_stack[ROW_MASK:ROW_MASK + 1, c, :, :, :].rearrange("p g r t -> p (g r) t"),
                             ones_row[:, :].unsqueeze(1).to_broadcast([1, 2 * G, CH])).then_inc(s_stack[c], 16)
                for j in range(3):
                    sp.wait_ge(*((s_part0[0], BC * (c + 1)), (s_split[0], c + 1), (s_last[0], c + 1))[j])
                    n, first = 3 - j, Q_PARTS.index(j)
                    sp.dma_start(q_rows[:, first:first + n, tok],
                                 parts[:, c % 2, 0, j:j + 1, :].to_broadcast([C, n, CH])).then_inc(s_qw[c % 2], 16)
                    sp.wait_ge((s_part0, s_split, s_last)[j][1], c + 1)
                    n, first = j + 1, (5, 3, 0)[j]
                    sp.dma_start(k_rows[:, first:first + n, tok], parts[:, c % 2, 1, 0:n, :]).then_inc(s_kw[c % 2], 16)
                sp.wait_ge(s_qw[c % 2], 48 * (c // 2 + 1))
                for par in range(2):
                    rows = q_rows[:, :, tok].rearrange("(g r d) s t -> r (d s) g t", r=2, d=D)
                    sp.dma_start(q_stack[par * HEAD_ROWS:(par + 1) * HEAD_ROWS, c, :, par, :],
                                 rows[par]).then_inc(s_stack[c], 16)
                sp.wait_ge(s_kw[c % 2], 48 * (c // 2 + 1))
                sp.dma_start(k_stack[0:2 * HEAD_ROWS, c, :, :],
                             k_rows[:, :, tok].rearrange("(g e) s t -> (e s) g t", e=2 * D)).then_inc(s_stack[c], 16)

            for k in range(HALVES):
                b, half = divmod(k, 2)
                sp.wait_ge(s_od, k + 1)
                dst = o_rows[b, 8 * half:8 * half + 8, :, :].rearrange("(q j) r t -> (j r) q t", j=4)
                sp.dma_start(dst, o_sb[:, k % 2, :].rearrange("r (q t) -> r q t", q=2)).then_inc(s_ow[k % 2], 16)
                if half:
                    for i in range(2):
                        sp.wait_ge(s_ow[i], 16 * (b + 1))
                    c, at = divmod(b, BC)
                    sp.dma_start(o_num[:, c, at * N:(at + 1) * N], o_rows[b, :, 0:D, :]).then_inc(s_or[c], 16)
                    sp.dma_start(o_den[:, c, at * N:(at + 1) * N],
                                 o_rows[b, :, D:D + 1, :].to_broadcast([H, D, N])).then_inc(s_or[c], 16)
            for b in range(B):
                c, at = b // BC, (b % BC) * N
                sp.wait_ge(s_out, b + 1)
                sp.dma_start(out_t[:, b * N:(b + 1) * N], out_sb[:, c, at:at + N]).then_inc(s_store, 16)
            sp.wait_ge(s_store, 16 * B)

        @block.gpsimd
        def _(pool):
            nc.gpsimd.memset(mean_w[:, :], 1.0 / C).then_inc(s_const, 1)
            nc.gpsimd.memset(ident[:, :], 0.0).then_inc(s_const, 1)
            nc.gpsimd.memset(eye8[:, :], 0.0).then_inc(s_const, 1)
            pool.wait_ge(s_const, 3)
            nc.gpsimd.affine_select(out=eye8[:, :], in_=eye8[:, :], compare_op=ALU.not_equal, fill=1.0, base=0,
                                    pattern=[[-1, B]], channel_multiplier=1).then_inc(s_const, 1)
            nc.gpsimd.affine_select(out=ident[:, :], in_=ident[:, :], compare_op=ALU.not_equal, fill=1.0, base=0,
                                    pattern=[[-1, C]], channel_multiplier=1).then_inc(s_const, 1)
            nc.gpsimd.memset(ones[:, :], 1.0).then_inc(s_const, 1)
            nc.gpsimd.memset(ones_row[:, :], 1.0).then_inc(s_const, 1)
            nc.gpsimd.memset(zero_row[:, :], 0.0).then_inc(s_const, 1)
            nc.gpsimd.memset(v_all[:, :, :, :, D:VW], 1.0).then_inc(s_const, 1)

            for c in range(1, NC):
                nc.gpsimd.memset(k_stack[:, c, :, :].rearrange("p g t -> p (g t)").bitcast(U32), ONES_BF16)\
                  .then_inc(s_fill, 1)
                nc.gpsimd.memset(q_stack[:, c, :, :, :].rearrange("p g r t -> p (g r t)").bitcast(U32), 0)\
                  .then_inc(s_fill, 1)

            def third_parts(c):
                for i in range(2):
                    if c >= 2:
                        pool.wait_ge((s_qw, s_kw)[i][c % 2], 48 * (c // 2))
                    pool.wait_ge(s_split[i], c + 1)
                    nc.gpsimd.tensor_tensor(parts[:, c % 2, i, 2, :], rest[:, c % 2, i, :], parts[:, c % 2, i, 1, :],
                                            ALU.subtract).then_inc(s_last[i], 1)

            third_parts(1)
            third_parts(2)
            for k in range(HALVES):
                pool.wait_ge(s_ad, item("scores", 4 * k + 3, 1) + 1)
                if k >= 2:
                    pool.wait_ge(s_a, item("turn", k - 2) + 1)
                neg = neg_max[:, k % 2, :, :, :]
                nc.gpsimd.tensor_copy(max_parts[:, k % 2, :, 0, :, :], neg).then_inc(s_mp, 1)
                pool.wait_ge(s_mp, 2 * k + 1)
                nc.gpsimd.tensor_tensor(max_parts[:, k % 2, :, 1, :, :], neg, max_parts[:, k % 2, :, 0, :, :],
                                        ALU.subtract).then_inc(s_mp, 1)
                pool.wait_ge(s_ad, item("turn", k) + 1)
                c, at = divmod(k // 2, BC)
                q0 = 4 * (k % 2)
                pool.dma_start(q_stack[ROW_MAX:ROW_MAX + 2, c, q0:q0 + 4, :, at * N:(at + 1) * N]
                               .rearrange("j g r t -> j (g r) t"), max_rows[:, k % 2, :]).then_inc(s_mr[k % 2], 16)
                if k == 0:
                    third_parts(3)
                if 6 <= k < 12:
                    i, second = divmod(k - 6, 2)
                    w = w_mlp[:, i * CH:(i + 1) * CH]
                    if k == 6:
                        pool.wait_ge(s_wb, 16)
                    if second:
                        pool.wait_ge(s_w_parts, 2 * i + 1)
                        nc.gpsimd.tensor_tensor(w_parts[:, 3 + i, :], w, w_parts[:, i, :].bitcast(F32),
                                                ALU.subtract).then_inc(s_w_parts, 1)
                    else:
                        nc.gpsimd.tensor_copy(w_parts[:, i, :], w).then_inc(s_w_parts, 1)

            for n in range(SPLIT_PAIRS):
                pool.wait_ge(s_gated_hi, n + 1)
                if n >= GB:
                    pool.wait_ge(s_w2, n - GB + 1)
                nc.gpsimd.tensor_tensor(gated_lo[:, n % GB, :], gated[:, n % GB, :], gated_hi[:, n % GB, :].bitcast(F32),
                                        ALU.subtract).then_inc(s_gated_lo, 1)

        @block.tensor
        def _(pe):
            def scale_and_shift():
                pe.wait_ge(s_wa, 16)
                pe.wait_ge(s_cond, 3)
                nc.tensor.matmul(bank[:, 0, 0:B], scale_w, cond[:, :], start=True, stop=True)
                nc.tensor.matmul(bank[:, 1, 0:B], shift_w, cond[:, :], start=True, stop=True).then_inc(s_small, 1)

            def flags_by_channel():
                pe.wait_ge(s_const, 6)
                pe.wait_ge(s_mask, 3)
                nc.tensor.matmul(bank[:, 2, 0:B], ones[:, :], any_diag[:, :], start=True, stop=True).then_inc(s_small, 1)

            def keep_clock(n):
                for _ in range(n):
                    nc.tensor.matmul(bank[:, 7, 0:C], mean_w[:, :], mean_w[:, :], start=True, stop=True)

            def mean_square(c):
                pe.wait_ge(s_sq, c + 1)
                if c >= 2:
                    pe.wait_ge(s_rs, c - 1)
                nc.tensor.matmul(bank[:, 3 + c % 2, :], mean_w[:, :], sq[:, c % 2, :],
                                 start=True, stop=True).then_inc(s_ss, 1)

            def q_and_k(c):
                pe.wait_ge(s_h, BC * (c + 1))
                for i in range(2):
                    if c >= 1:
                        pe.wait_ge(s_rest[i], (BC, 1)[i] * c)
                    nc.tensor.matmul(bank[:, 5 + i, :], qkv_w[:, i * C:(i + 1) * C], h[:, c % 2, :],
                                     start=True, stop=True).then_inc(s_qk, 1)

            def values(c):
                if c >= 1:
                    pe.wait_ge(s_v_out, c)
                for t in range(CH // C):
                    mm = nc.tensor.matmul(bank[:, 7, t * C:(t + 1) * C], h[:, c % 2, t * C:(t + 1) * C],
                                          qkv_w[:, 2 * C:3 * C], start=True, stop=True)
                mm.then_inc(s_v, 1)

            def ring_bank(n):
                if n >= RING:
                    pe.wait_ge(s_ad, n - RING + 1)
                return bank[:, n % RING, :]

            def query_scores(u, par):
                b, g = divmod(u, G)
                c, at = b // BC, (b % BC) * N
                if u % (BC * G) == 0 and par == 0:
                    pe.wait_ge(s_stack[c], 16 * 6)
                scores = ring_bank(item("scores", u, par))
                for t in range(KT):
                    mm = nc.tensor.matmul(scores[:, t * N:(t + 1) * N],
                                          q_stack[:, c, g, par, at + t * 128:at + (t + 1) * 128],
                                          k_stack[:, c, g, at:at + N], start=True, stop=True)
                mm.then_inc(s_a, 1)

            def turn_maxima(k):
                turned = ring_bank(item("turn", k))
                pe.wait_ge(s_mp, 2 * (k + 1))
                for t in range(KT):
                    mm = nc.tensor.transpose(turned[0:2 * G, t * 64:(t + 1) * 64].bitcast(BF16),
                                             max_parts[:, k % 2, t, :, :, :].rearrange("p j g r -> p (j g r)"),
                                             ident[:, :])
                mm.then_inc(s_a, 1)

            def project(c):
                projected = ring_bank(item("project", c))
                if c == 0:
                    pe.wait_ge(s_wb, 16)
                pe.wait_ge(s_on, c + 1)
                nc.tensor.matmul(projected, proj_w, o_num[:, c, :], start=True, stop=True).then_inc(s_a, 1)

            def mean_square_2(c):
                squares = ring_bank(item("square", c))
                pe.wait_ge(s_sq2, c + 1)
                nc.tensor.matmul(squares, mean_w[:, :], sq2[:, c % 2, :], start=True, stop=True).then_inc(s_a, 1)

            def zero_outputs():
                pe.wait_ge(s_const, 8)
                pe.wait_ge(s_rest[1], NC)
                pe.wait_ge(s_v_out, NC)
                for i in range(2):
                    nc.tensor.matmul(bank[:, 6 + i, :], zero_row[:, :], ones_row[:, :], start=True, stop=True)

            def key_scores(u, par):
                b, g = divmod(u, G)
                c, at = b // BC, (b % BC) * N
                v = 2 * u + par
                if v % 8 == 0:
                    k = u // 4
                    pe.wait_ge(s_mr[k % 2], 16 * (k // 2 + 1))
                if v >= RING:
                    pe.wait_ge(s_e, v - RING + 1)
                for t in range(KT):
                    mm = nc.tensor.matmul(bank[:, RING + v % RING, t * N:(t + 1) * N],
                                          k_stack[:, c, g, at + t * 128:at + (t + 1) * 128],
                                          q_stack[:, c, g, par, at:at + N], start=True, stop=True)
                mm.then_inc(s_b, 1)

            def p_times_v(q, t):
                b, g = divmod(2 * q, G)
                k = q // 2
                if t == 0:
                    pe.wait_ge(s_e, 4 * q + 4)
                    if q == 0:
                        pe.wait_ge(s_const, 9)
                    if q % 2 == 0 and k >= 2:
                        pe.wait_ge(s_od, k - 1)
                for j in range(4):
                    mm = nc.tensor.matmul(bank[32 * j:32 * j + VW, 6 + k % 2, (q % 2) * N:(q % 2 + 1) * N],
                                          v_all[:, b, t, 2 * g + j, :],
                                          p_exp[:, (2 * q + j // 2) % 4, j % 2, t, :],
                                          start=(t == 0), stop=(t == KT - 1), tile_position=(0, 32 * j))
                if t == KT - 1:
                    mm.then_inc(s_pv, 1)

            def slot_banks(what):
                j = SLOTS_MLP.index(what)
                if j >= 3:
                    before = SLOTS_MLP[j - 3]
                    if before == "project":
                        pe.wait_ge(s_y3, 1)
                    elif before == "square":
                        pe.wait_ge(s_rs3, 1)
                    else:
                        pe.wait_ge(s_gated, before + 1)
                return [bank[:, 2 * (j % 3) + i, :] for i in range(2)]

            def project_last():
                out = slot_banks("project")[0]
                pe.wait_ge(s_on, NC)
                nc.tensor.matmul(out, proj_w, o_num[:, NC - 1, :], start=True, stop=True).then_inc(s_proj, 1)

            def mean_square_last():
                out = slot_banks("square")[0]
                pe.wait_ge(s_sq2, NC)
                nc.tensor.matmul(out, mean_w[:, :], sq2[:, (NC - 1) % 2, :], start=True, stop=True).then_inc(s_ss2, 1)

            def mlp_in(n):
                c, m = divmod(n, MT)
                if m == 0:
                    pe.wait_ge(s_h2, BC * (c + 1))
                    pe.wait_ge(s_h2_lo, BC * (c + 1))
                if n == 0:
                    pe.wait_ge(s_w_parts, 6)
                    pe.wait_ge(s_ad, len(ITEMS))
                if n == 1:
                    pe.wait_ge(s_e, 2 * UNITS)
                for i, out in enumerate(slot_banks(n)):
                    w_hi, w_lo = (w_parts[:, 3 * j + i, m * C:(m + 1) * C] for j in range(2))
                    nc.tensor.matmul(out, w_hi, h2_hi[:, c, :], start=True, stop=False)
                    nc.tensor.matmul(out, w_hi, h2_lo[:, c, :], start=False, stop=False)
                    nc.tensor.matmul(out, w_lo, h2_hi[:, c, :], start=False, stop=True).then_inc(s_w1, 1)

            def mlp_out(n):
                c, m = divmod(n, MT)
                pe.wait_ge(*((s_gated_hi, n + 1) if n < SPLIT_PAIRS else (s_gated, n + 1)))
                if n == 0:
                    pe.wait_ge(s_od, HALVES)
                if m == 0 and c >= 2:
                    pe.wait_ge(s_out, BC * (c - 1))
                out = bank[:, 6 + c % 2, :]
                if n >= SPLIT_PAIRS:
                    nc.tensor.matmul(out, w_mlp[:, 2 * MLP + m * C:2 * MLP + (m + 1) * C], gated[:, n % GB, :],
                                     start=False, stop=(m == MT - 1)).then_inc(s_w2, 1)
                    return
                w_hi, w_lo = (w_parts[:, 3 * j + 2, m * C:(m + 1) * C] for j in range(2))
                nc.tensor.matmul(out, w_hi, gated_hi[:, n % GB, :], start=(m == 0), stop=False)
                nc.tensor.matmul(out, w_lo, gated_hi[:, n % GB, :], start=False, stop=False)
                pe.wait_ge(s_gated_lo, n + 1)
                nc.tensor.matmul(out, w_hi, gated_lo[:, n % GB, :], start=False, stop=(m == MT - 1)).then_inc(s_w2, 1)

            pe.wait_ge(s_const, 1)
            keep_clock(WARM[0])
            mean_square(0)
            scale_and_shift()
            mean_square(1)
            flags_by_channel()
            keep_clock(WARM[1])
            mean_square(2)
            q_and_k(0)
            values(0)
            mean_square(3)
            q_and_k(1)
            values(1)
            q_and_k(2)
            values(2)
            q_and_k(3)
            for p in range(UNITS + LEAD):
                u = p - LEAD
                if p < UNITS:
                    query_scores(p, 0)
                if u >= 0:
                    key_scores(u, 0)
                if p < UNITS:
                    query_scores(p, 1)
                if u >= 0:
                    key_scores(u, 1)
                if p == 2:
                    values(3)
                if u == 0:
                    zero_outputs()
                if u >= LAG:
                    p_times_v((u - LAG) // 2, (u - LAG) % 2)
                if p % 4 == 0 and 4 <= p <= UNITS:
                    turn_maxima(p // 4 - 1)
                for c in range(NC - 1):
                    if p == project_position(c):
                        project(c)
                    if p == square_position(c):
                        mean_square_2(c)
            mlp_in(0)
            for u in range(UNITS - LAG, UNITS):
                p_times_v(u // 2, u % 2)

            for n in range(NC * MT + OUT_LAG):
                if 1 <= n < NC * MT:
                    mlp_in(n)
                if n >= OUT_LAG:
                    mlp_out(n - OUT_LAG)
                if n == AT_PROJECT:
                    project_last()
                if n == AT_MEAN:
                    mean_square_last()

        @block.scalar
        def _(act):
            nc.scalar.preload_act_table_set("natural_log_exp_and_others")

            def square(c):
                act.wait_ge(s_x[c], 16)
                if c >= 2:
                    act.wait_ge(s_ss, c - 1)
                nc.scalar.activation(sq[:, c % 2, :], x_sb[:, c * CH:(c + 1) * CH], ACT.Square).then_inc(s_sq, 1)

            def logarithm(t, s):
                nc.scalar.activation(t, t, ACT.Ln).then_inc(s, 1)

            def power_of_logarithm(t, exponent, s, n):
                act.wait_ge(s, n)
                nc.scalar.activation(t, t, ACT.Exp, scale=exponent).then_inc(s, 1)

            def inverse_norm(c):
                act.wait_ge(s_rs, c + 1)
                logarithm(rs[:, c, :], s_inv)
                power_of_logarithm(rs[:, c, :], -0.5, s_inv, 2 * c + 1)

            def shifted(c):
                for b in range(BC * c, BC * c + BC):
                    at = (b % BC) * N
                    act.wait_ge(s_xn, b + 1)
                    if c >= 2:
                        act.wait_ge(s_v, c - 1)
                    nc.scalar.activation(h[:, c % 2, at:at + N], xn[:, c % 2, at:at + N], ACT.Identity,
                                         bias=shift[:, b:b + 1]).then_inc(s_h, 1)

            def first_parts(c):
                if c >= 2:
                    act.wait_ge(s_qw[c % 2], 48 * (c // 2))
                    act.wait_ge(s_kw[c % 2], 48 * (c // 2))
                act.wait_ge(s_qk, 2 * c + 1)
                for i in range(BC):
                    nc.scalar.activation(parts[:, c % 2, 0, 0, i * N:(i + 1) * N], bank[:, 5, i * N:(i + 1) * N],
                                         ACT.Copy, scale=any_all[:, BC * c + i:BC * c + i + 1]).then_inc(s_part0[0], 1)
                act.wait_ge(s_qk, 2 * c + 2)
                nc.scalar.activation(parts[:, c % 2, 1, 0, :], bank[:, 6, :], ACT.Copy).then_inc(s_part0[1], 1)

            def values(c):
                act.wait_ge(s_v, c + 1)
                nc.scalar.activation(v_all[:, BC * c:BC * (c + 1), :, :, 0:D],
                                     bank[:, 7, :].rearrange("p (b t h d) -> p b t h d", b=BC, t=KT, h=H),
                                     ACT.Copy).then_inc(s_v_out, 1)

            square(0)
            act.wait_ge(s_in, 32)
            nc.scalar.activation(sig[:, :], c_sb, ACT.Exp, scale=-1.0).then_inc(s_sig, 1)
            square(1)
            inverse_norm(0)
            square(2)
            act.wait_ge(s_shift, 1)
            shifted(0)
            inverse_norm(1)
            act.wait_ge(s_any, 1)
            first_parts(0)
            shifted(1)
            square(3)
            inverse_norm(2)
            values(0)
            shifted(2)
            first_parts(1)
            values(1)
            inverse_norm(3)
            shifted(3)
            first_parts(2)
            values(2)
            first_parts(3)
            values(3)

            def drain_output(k):
                act.wait_ge(s_pv, 2 * k + 2)
                if k >= 2:
                    act.wait_ge(s_ow[k % 2], 16 * (k // 2))
                nc.scalar.activation(o_sb[:, k % 2, :], bank[:, 6 + k % 2, :], ACT.Copy).then_inc(s_od, 1)

            def ln_sum(c):
                act.wait_ge(s_or[c], 32 * BC)
                logarithm(o_den[:, c, :], s_rec)

            def inverse_sum(c):
                power_of_logarithm(o_den[:, c, :], -1.0, s_rec, 2 * c + 1)

            def square_2(c):
                act.wait_ge(*((s_ad, item("project", c) + 1) if c < NC - 1 else (s_y3, 1)))
                if c == NC - 1:
                    act.wait_ge(s_a, item("square", c - 2) + 1)
                nc.scalar.activation(sq2[:, c % 2, :], y[:, c, :], ACT.Square).then_inc(s_sq2, 1)

            def ln_norm_2(c):
                act.wait_ge(*((s_ad, item("square", c) + 1) if c < NC - 1 else (s_rs3, 1)))
                logarithm(rs2[:, c, :], s_inv2)

            def inverse_norm_2(c):
                power_of_logarithm(rs2[:, c, :], -0.5, s_inv2, 2 * c + 1)

            def shifted_2(c):
                for b in range(BC * c, BC * c + BC):
                    at = (b % BC) * N
                    act.wait_ge(s_xn2, b + 1)
                    nc.scalar.activation(h2_hi[:, c, at:at + N], xn2[:, c, at:at + N], ACT.Identity,
                                         bias=shift[:, b:b + 1]).then_inc(s_h2, 1)

            for u in range(UNITS):
                if u >= 4:
                    act.wait_ge(s_pv, u // 2 - 1)
                for par in range(2):
                    v = 2 * u + par
                    act.wait_ge(s_b, v + 1)
                    nc.scalar.activation(p_exp[:, u % 4, par, :, :],
                                         bank[:, RING + v % RING, :].rearrange("p (t q) -> p t q", t=KT),
                                         ACT.Exp, scale=D ** -0.5).then_inc(s_e, 1)
                if u % 4 == 2 and 6 <= u < UNITS - 2:
                    drain_output(u // 4 - 1)
                for c in range(NC - 1):
                    behind = u - BC * G * (c + 1)
                    if behind == P_LN_SUM:
                        ln_sum(c)
                    if behind == P_INVERSE_SUM:
                        inverse_sum(c)
                    if c < NC - 2 and behind == P_SQUARE:
                        square_2(c)
                    if c < NC - 2 and behind == P_LN_NORM:
                        ln_norm_2(c)
                    if c < NC - 2 and behind == P_INVERSE_NORM:
                        inverse_norm_2(c)
                    if c < NC - 2 and behind == P_SHIFT:
                        shifted_2(c)

            def first_part_gated(n):
                act.wait_ge(s_gated, n + 1)
                if n >= GB:
                    act.wait_ge(s_w2, n - GB + 1)
                nc.scalar.activation(gated_hi[:, n % GB, :], gated[:, n % GB, :], ACT.Copy).then_inc(s_gated_hi, 1)

            for n in range(NC * MT):
                m = n % MT
                act.wait_ge(s_w1, 2 * n + 1)
                if n >= 2:
                    act.wait_ge(s_silu, n - 1)
                nc.scalar.activation(sig_x1[:, n % 2, :], bank[:, 2 * (SLOTS_MLP.index(n) % 3), :], ACT.Sigmoid,
                                     bias=vec[:, V_B1 + m:V_B1 + m + 1]).then_inc(s_sig_x1, 1)
                if 1 <= n <= SPLIT_PAIRS:
                    first_part_gated(n - 1)
                if n == AT_INVERSE_SUM:
                    nc.scalar.preload_act_table_set("natural_log_exp_and_others")
                    ln_norm_2(NC - 2)
                    ln_sum(NC - 1)
                    inverse_norm_2(NC - 2)
                    inverse_sum(NC - 1)
                if n == AT_INVERSE_SUM + 1:
                    shifted_2(NC - 2)
                if n == AT_SQUARE:
                    square_2(NC - 1)
                if n == AT_INVERSE_NORM:
                    nc.scalar.preload_act_table_set("natural_log_exp_and_others")
                    ln_norm_2(NC - 1)
                    inverse_norm_2(NC - 1)
                if n == AT_SHIFT:
                    shifted_2(NC - 1)

        @block.vector
        def _(dve):
            nc.vector.memset(words[:, 0:1].bitcast(U32), ONES_BF16).then_inc(s_words, 1)
            nc.vector.memset(words[:, 1:2], 0.0).then_inc(s_words, 1)
            dve.wait_ge(s_words, 2)
            def words_of(rows):
                return rows.bitcast(F32).rearrange("p (s t) -> p s t", t=CH)

            word = words[:, 0:1].unsqueeze(2).to_broadcast([C, 4, CH])
            nc.vector.tensor_copy(words_of(k_stack[:, 0, :, :].rearrange("p g t -> p (g t)")), word).then_inc(s_fill0, 1)
            word = words[:, 1:2].unsqueeze(2).to_broadcast([C, 4, CH])
            for i in range(2):
                half_stack = q_stack[:, 0, i * G // 2:(i + 1) * G // 2, :, :].rearrange("p g r t -> p (g r t)")
                nc.vector.tensor_copy(words_of(half_stack), word).then_inc(s_fill0, 1)

            dve.wait_ge(s_in, 32)
            dve.wait_ge(s_sig, 1)
            nc.vector.tensor_scalar(sig[:, :], sig[:, :], 1.0, None, ALU.add).then_inc(s_cond, 1)
            dve.wait_ge(s_cond, 1)
            nc.vector.reciprocal(sig[:, :], sig[:, :]).then_inc(s_cond, 1)
            dve.wait_ge(s_cond, 2)
            nc.vector.tensor_tensor(cond[:, :], c_sb, sig[:, :], ALU.mult).then_inc(s_cond, 1)

            def flags():
                nc.vector.tensor_scalar(valid[:, :], mask_sb[:, :], 0.0, None, ALU.not_equal).then_inc(s_mask, 1)
                dve.wait_ge(s_mask, 1)
                nc.vector.tensor_reduce(out=any_valid[:, :], in_=valid[:, :], axis=AX.X, op=ALU.max).then_inc(s_mask, 1)
                dve.wait_ge(s_mask, 2)
                dve.wait_ge(s_const, 5)
                nc.vector.tensor_scalar(any_diag[:, :], eye8[:, :], any_valid[:, :], None, ALU.mult).then_inc(s_mask, 1)

            def gains():
                dve.wait_ge(s_small, 1)
                nc.vector.tensor_scalar(gain[:, :], bank[:, 0, 0:B], vec[:, V_SCALE_B:V_SCALE_B + 1], 1.0,
                                        ALU.add, ALU.add).then_inc(s_gain, 1)
                nc.vector.tensor_scalar(shift[:, :], bank[:, 1, 0:B], vec[:, V_SHIFT_B:V_SHIFT_B + 1], None,
                                        ALU.add).then_inc(s_shift, 1)
                dve.wait_ge(s_gain, 1)
                nc.vector.tensor_scalar(gain[:, :], gain[:, :], 0.1, 10.0, ALU.max, ALU.min).then_inc(s_gain, 1)
                dve.wait_ge(s_gain, 2)
                nc.vector.tensor_scalar(gain[:, :], gain[:, :], vec[:, V_NORM:V_NORM + 1], None,
                                        ALU.mult).then_inc(s_gain, 1)

            def added_to_masked():
                nc.vector.tensor_scalar(valid[:, :], valid[:, :], 1.0, -MASKED, ALU.subtract, ALU.mult).then_inc(s_mask, 1)
                dve.wait_ge(s_mask, 4)
                nc.vector.tensor_scalar(mask_add[:, :], valid[:, :], any_valid[:, :], None, ALU.mult).then_inc(s_mask, 1)

            def guard(c):
                dve.wait_ge(s_ss, c + 1)
                nc.vector.tensor_scalar(rs[:, c, :], bank[:, 3 + c % 2, :], EPS * EPS, None,
                                        ALU.max).then_inc(s_rs, 1)

            def norm(c):
                if c == 0:
                    dve.wait_ge(s_gain, 3)
                dve.wait_ge(s_inv, 2 * c + 2)
                for i in range(BC):
                    b = BC * c + i
                    if c >= 2:
                        dve.wait_ge(s_h, b - 3)
                    nc.vector.scalar_tensor_tensor(out=xn[:, c % 2, i * N:(i + 1) * N],
                                                   in0=x_sb[:, b * N:(b + 1) * N], scalar=gain[:, b:b + 1],
                                                   in1=rs[:, c, i * N:(i + 1) * N],
                                                   op0=ALU.mult, op1=ALU.mult).then_inc(s_xn, 1)

            def split(c):
                q_part, k_part, rest_q, rest_k = parts[:, c % 2, 0, :, :], parts[:, c % 2, 1, :, :], *(
                    rest[:, c % 2, i, :] for i in range(2))
                if c >= 2:
                    for s in s_last:
                        dve.wait_ge(s, c - 1)
                dve.wait_ge(s_part0[0], BC * (c + 1))
                for i in range(BC):
                    at = slice(i * N, (i + 1) * N)
                    nc.vector.scalar_tensor_tensor(out=rest_q[:, at], in0=bank[:, 5, at],
                                                   scalar=any_all[:, BC * c + i:BC * c + i + 1], in1=q_part[:, 0, at],
                                                   op0=ALU.mult, op1=ALU.subtract).then_inc(s_rest[0], 1)
                dve.wait_ge(s_part0[1], c + 1)
                nc.vector.tensor_tensor(rest_k, bank[:, 6, :], k_part[:, 0, :], ALU.subtract).then_inc(s_rest[1], 1)
                dve.wait_ge(s_rest[0], BC * (c + 1))
                nc.vector.tensor_copy(q_part[:, 1, :], rest_q).then_inc(s_split[0], 1)
                dve.wait_ge(s_rest[1], c + 1)
                nc.vector.tensor_copy(k_part[:, 1, :], rest_k).then_inc(s_split[1], 1)
                if c == 0:
                    dve.wait_ge(s_split[0], 1)
                    nc.vector.tensor_tensor(q_part[:, 2, :], rest_q, q_part[:, 1, :], ALU.subtract).then_inc(s_last[0], 1)
                    dve.wait_ge(s_split[1], 1)
                    nc.vector.tensor_tensor(k_part[:, 2, :], rest_k, k_part[:, 1, :], ALU.subtract).then_inc(s_last[1], 1)

            def maxima(u):
                k, g = divmod(u, 4)
                if g == 0 and k >= 2:
                    dve.wait_ge(s_mp, 2 * (k - 1))
                for par in range(2):
                    n = item("scores", u, par)
                    dve.wait_ge(s_a, n + 1)
                    nc.vector.tensor_reduce(out=neg_max[:, k % 2, :, g, par],
                                            in_=bank[:, n % RING, :].rearrange("p (t k) -> p t k", t=KT),
                                            axis=AX.X, op=ALU.max, negate=True).then_inc(s_ad, 1)

            def turned(k):
                n = item("turn", k)
                dve.wait_ge(s_a, n + 1)
                if k >= 2:
                    dve.wait_ge(s_mr[k % 2], 16 * (k // 2))
                nc.vector.tensor_copy(max_rows[:, k % 2, :],
                                      bank[0:2 * G, n % RING, 0:2 * 64].bitcast(BF16)).then_inc(s_ad, 1)

            def drain_output(k):
                dve.wait_ge(s_pv, 2 * k + 2)
                dve.wait_ge(s_od, k)
                dve.wait_ge(s_ow[k % 2], 16 * (k // 2))
                nc.vector.tensor_copy(o_sb[:, k % 2, :], bank[:, 6 + k % 2, :]).then_inc(s_od, 1)

            def over_sum(c):
                dve.wait_ge(s_rec, 2 * c + 2)
                nc.vector.tensor_tensor(o_num[:, c, :], o_num[:, c, :], o_den[:, c, :], ALU.mult).then_inc(s_on, 1)

            def residual(c, at, done):
                nc.vector.scalar_tensor_tensor(out=y[:, c, :], in0=bank[:, at, :],
                                               scalar=vec[:, V_PROJ_B:V_PROJ_B + 1],
                                               in1=x_sb[:, c * CH:(c + 1) * CH], op0=ALU.add,
                                               op1=ALU.add).then_inc(done, 1)

            def guard_2(c, at, done):
                nc.vector.tensor_scalar(rs2[:, c, :], bank[:, at, :], EPS * EPS, None, ALU.max).then_inc(done, 1)

            def norm_2(c):
                dve.wait_ge(s_inv2, 2 * c + 2)
                for i in range(BC):
                    b = BC * c + i
                    nc.vector.scalar_tensor_tensor(out=xn2[:, c, i * N:(i + 1) * N],
                                                   in0=y[:, c, i * N:(i + 1) * N], scalar=gain[:, b:b + 1],
                                                   in1=rs2[:, c, i * N:(i + 1) * N],
                                                   op0=ALU.mult, op1=ALU.mult).then_inc(s_xn2, 1)

            def second_part_h2(c):
                for i in range(BC):
                    b = BC * c + i
                    at = slice(i * N, (i + 1) * N)
                    dve.wait_ge(s_h2, b + 1)
                    nc.vector.scalar_tensor_tensor(out=h2_lo[:, c, at], in0=xn2[:, c, at], scalar=shift[:, b:b + 1],
                                                   in1=h2_hi[:, c, at].bitcast(F32), op0=ALU.add,
                                                   op1=ALU.subtract).then_inc(s_h2_lo, 1)

            def add_out(c):
                dve.wait_ge(s_w2, MT * (c + 1))
                for at in range(0, CH, N):
                    nc.vector.scalar_tensor_tensor(out=out_sb[:, c, at:at + N], in0=bank[:, 6 + c % 2, at:at + N],
                                                   scalar=vec[:, V_B2:V_B2 + 1], in1=y[:, c, at:at + N],
                                                   op0=ALU.add, op1=ALU.add).then_inc(s_out, 1)

            guard(0)
            gains()
            flags()
            norm(0)
            guard(1)
            dve.wait_ge(s_small, 2)
            nc.vector.tensor_copy(any_all[:, :], bank[:, 2, 0:B]).then_inc(s_any, 1)
            guard(2)
            norm(1)
            added_to_masked()
            split(0)
            norm(2)
            guard(3)
            split(1)
            norm(3)
            split(2)
            for p in range(UNITS + LEAD):
                if p < UNITS:
                    maxima(p)
                if p % 4 == 0 and 4 <= p <= UNITS:
                    turned(p // 4 - 1)
                if p == 4:
                    split(3)
                if p == UNITS - 2 + LEAD:
                    drain_output(HALVES - 2)
                for c in range(NC - 1):
                    behind = p - LEAD - BC * G * (c + 1)
                    if behind == P_OVER_SUM:
                        over_sum(c)
                    if p == project_position(c):
                        n = item("project", c)
                        dve.wait_ge(s_a, n + 1)
                        residual(c, n % RING, s_ad)
                    if c == NC - 2 and p == project_position(c) + 1:
                        dve.wait_ge(s_ad, item("project", c) + 1)
                        nc.vector.tensor_tensor(sq2[:, c % 2, :], y[:, c, :], y[:, c, :], ALU.mult).then_inc(s_sq2, 1)
                    if p == square_position(c):
                        n = item("square", c)
                        dve.wait_ge(s_a, n + 1)
                        guard_2(c, n % RING, s_ad)
                    if c < NC - 2 and behind == P_NORM:
                        norm_2(c)
                    if c < NC - 2 and behind == P_SECOND_PART:
                        second_part_h2(c)
            drain_output(HALVES - 1)

            for n in range(NC * MT):
                c, m = divmod(n, MT)
                first = 2 * (SLOTS_MLP.index(n) % 3)
                dve.wait_ge(s_sig_x1, n + 1)
                nc.vector.scalar_tensor_tensor(out=silu[:, n % 2, :], in0=bank[:, first, :],
                                               scalar=vec[:, V_B1 + m:V_B1 + m + 1], in1=sig_x1[:, n % 2, :],
                                               op0=ALU.add, op1=ALU.mult).then_inc(s_silu, 1)
                dve.wait_ge(s_silu, n + 1)
                dve.wait_ge(s_w1, 2 * n + 2)
                if n >= GB:
                    dve.wait_ge(s_gated_lo, n - GB + 1)
                b1 = vec[:, V_B1 + MT + m:V_B1 + MT + m + 1]
                nc.vector.scalar_tensor_tensor(out=gated[:, n % GB, :], in0=bank[:, first + 1, :], scalar=b1,
                                               in1=silu[:, n % 2, :], op0=ALU.add, op1=ALU.mult).then_inc(s_gated, 1)
                if n == AT_INVERSE_SUM + 2:
                    second_part_h2(NC - 2)
                if n == AT_OVER_SUM:
                    norm_2(NC - 2)
                    over_sum(NC - 1)
                if n == AT_RESIDUAL:
                    dve.wait_ge(s_proj, 1)
                    residual(NC - 1, 2 * (SLOTS_MLP.index("project") % 3), s_y3)
                if n == AT_GUARD:
                    dve.wait_ge(s_ss2, 1)
                    guard_2(NC - 1, 2 * (SLOTS_MLP.index("square") % 3), s_rs3)
                if n == AT_NORM:
                    norm_2(NC - 1)
                if n == AT_SECOND_PART:
                    second_part_h2(NC - 1)
                if m == OUT_LAG and c >= 1:
                    add_out(c - 1)
            add_out(NC - 1)


def kernel(x, cond_1024, mask_BxS_ik0, L0_cond_norm_w, L0_cond_scale_w, L0_cond_scale_b, L0_cond_shift_w,
           L0_cond_shift_b, L0_cond_qkv_w, L0_cond_proj_w, L0_cond_proj_b, L0_cond_mlp_w1, L0_cond_mlp_b1,
           L0_cond_mlp_w2, L0_cond_mlp_b2):
    import numpy as np
    import concourse.bacc as bacc
    from concourse.bass_utils import run_bass_kernel_spmd

    def turned(a):
        return np.ascontiguousarray(np.asarray(a).T)

    vectors = [np.asarray(v).reshape(-1, C) for v in
               (L0_cond_norm_w, L0_cond_scale_b, L0_cond_shift_b, L0_cond_proj_b, L0_cond_mlp_b2, L0_cond_mlp_b1,
                cond_1024)]
    w2 = np.asarray(L0_cond_mlp_w2).T.reshape(MT, C, C).transpose(1, 0, 2).reshape(C, MLP)
    arrays = {
        "x_t": turned(np.asarray(x).reshape(TOK, C)),
        "small": turned(np.concatenate(vectors, axis=0)),
        "mask": np.ascontiguousarray(mask_BxS_ik0),
        "front_w": turned(np.concatenate([L0_cond_scale_w, L0_cond_shift_w, L0_cond_qkv_w], axis=0)),
        "back_w": np.concatenate([turned(L0_cond_proj_w), turned(L0_cond_mlp_w1), w2], axis=1),
    }
    nc = bacc.Bacc("TRN2", target_bir_lowering=False, num_devices=1)
    args = [nc.dram_tensor(name, a.shape, mybir.dt.from_np(a.dtype), kind="ExternalInput").ap()
            for name, a in arrays.items()]
    out_t = nc.dram_tensor("out_t", (C, TOK), F32, kind="ExternalOutput").ap()
    build(nc, *args, out_t)
    result = run_bass_kernel_spmd(nc, [arrays], core_ids=[0]).results[0]["out_t"]
    return np.ascontiguousarray(result.T).reshape(B, N, C)
```
